# Optimizing a Trainium2 kernel written in Bass

```python
import numpy as np
import jax
import jax.numpy as jnp

def _softmax(x, axis=-1):
    return jax.nn.softmax(x, axis=axis)

def _gelu(x):
    return jax.nn.gelu(x, approximate=True)

def _silu(x):
    return jax.nn.silu(x)

def _sigmoid(x):
    return jax.nn.sigmoid(x)

def _layernorm(x, axis=-1, eps=1e-05):
    m = jnp.mean(x, axis=axis, keepdims=True)
    v = jnp.var(x, axis=axis, keepdims=True)
    return (x - m) / jnp.sqrt(v + eps)

def _scatter_add(tgt, idx, src, axis=0):
    return tgt.at[idx].add(src)

def _segment_sum(src, seg, n):
    return jax.ops.segment_sum(src, seg, n)
kernel_name = 'mk_gnn_resnorm_d1_gnn_r8_71b971'

def setup_inputs(seed: int=0):
    np.random.seed(seed)
    _w = jnp.asarray

    def _rec_inputs():
        import jax
        import jax.numpy as jnp
        _gk = jax.random.key(seed)
        x = 0.0001712 + 1 * jax.random.normal(jax.random.fold_in(_gk, 1), (12500, 16), jnp.float32)
        _s = jax.random.randint(jax.random.fold_in(_gk, 2), (200000,), 0, 12500, jnp.int32)
        _d = jax.random.randint(jax.random.fold_in(_gk, 3), (200000,), 0, 12500, jnp.int32)
        _loop = jnp.arange(12500, dtype=jnp.int32)
        src = jnp.concatenate([_s, _d, _loop])
        dst = jnp.concatenate([_d, _s, _loop])
        _o = jnp.argsort(dst, stable=True)
        src = src[_o]
        dst = dst[_o]
        edge_attr_6 = jax.random.uniform(jax.random.fold_in(_gk, 11), (412500, 6), jnp.float32, 0.0, 1)
        return (x, src, dst, edge_attr_6)
    x, src, dst, edge_attr_6 = _rec_inputs()

    def _L0_gnn_setup():
        import jax, jax.numpy as jnp
        import numpy as np
        LATENT = 16
        KDIM = 128
        EDIM = 6
        DEPTH = 4
        N_NODES = 6250
        N_EDGES = 100000

        def _kernel_net(edge_attr, kW1, kb1, kW2, kb2, kW3, kb3):
            h = jax.nn.gelu(edge_attr @ kW1 + kb1)
            h = jax.nn.gelu(h @ kW2 + kb2)
            return h @ kW3 + kb3
        key = jax.random.key(seed)
        ks = jax.random.split(key, 12)
        inp = {'nodes': jax.random.normal(ks[0], (N_NODES, LATENT), dtype=jnp.float32), 'edge_index': jax.random.randint(ks[1], (2, N_EDGES), 0, N_NODES, dtype=jnp.int64), 'edge_attr': jax.random.uniform(ks[2], (N_EDGES, EDIM), dtype=jnp.float32), 'kW1': jax.random.normal(ks[3], (EDIM, KDIM), dtype=jnp.float32) / np.sqrt(EDIM), 'kb1': jnp.zeros((KDIM,), dtype=jnp.float32), 'kW2': jax.random.normal(ks[4], (KDIM, KDIM), dtype=jnp.float32) / np.sqrt(KDIM), 'kb2': jnp.zeros((KDIM,), dtype=jnp.float32), 'kW3': jax.random.normal(ks[5], (KDIM, LATENT * LATENT), dtype=jnp.float32) / np.sqrt(KDIM), 'kb3': jnp.zeros((LATENT * LATENT,), dtype=jnp.float32), 'root_W': jax.random.normal(ks[6], (DEPTH, LATENT, LATENT), dtype=jnp.float32) / np.sqrt(LATENT), 'root_b': jnp.zeros((DEPTH, LATENT), dtype=jnp.float32)}
        return inp
    _L0_gnn_all = _L0_gnn_setup()
    _L0_gnn_in = {k: v for k, v in _L0_gnn_all.items() if k in ('kW1', 'kb1', 'kW2', 'kb2', 'kW3', 'kb3', 'root_W', 'root_b')}
    del _L0_gnn_all
    return {'x': x, 'src': src, 'dst': dst, 'edge_attr_6': edge_attr_6, 'L0_gnn_kW1': _L0_gnn_in['kW1'], 'L0_gnn_kb1': _L0_gnn_in['kb1'], 'L0_gnn_kW2': _L0_gnn_in['kW2'], 'L0_gnn_kb2': _L0_gnn_in['kb2'], 'L0_gnn_kW3': _L0_gnn_in['kW3'], 'L0_gnn_kb3': _L0_gnn_in['kb3'], 'L0_gnn_root_W': _L0_gnn_in['root_W'], 'L0_gnn_root_b': _L0_gnn_in['root_b']}

def reference(x, src, dst, edge_attr_6, L0_gnn_kW1, L0_gnn_kb1, L0_gnn_kW2, L0_gnn_kb2, L0_gnn_kW3, L0_gnn_kb3, L0_gnn_root_W, L0_gnn_root_b):
    import jax
    import jax.numpy as jnp

    def _L0_gnn_ref(nodes, edge_attr, kW1, kb1, kW2, kb2, kW3, kb3, root_W, root_b, edge_index):
        import jax, jax.numpy as jnp
        import numpy as np
        LATENT = 16
        KDIM = 128
        EDIM = 6
        DEPTH = 4
        N_NODES = 6250
        N_EDGES = 100000

        def _kernel_net(edge_attr, kW1, kb1, kW2, kb2, kW3, kb3):
            h = jax.nn.gelu(edge_attr @ kW1 + kb1)
            h = jax.nn.gelu(h @ kW2 + kb2)
            return h @ kW3 + kb3
        src, dst = (edge_index[0], edge_index[1])
        n = nodes.shape[0]
        w = _kernel_net(edge_attr, kW1, kb1, kW2, kb2, kW3, kb3).reshape(-1, LATENT, LATENT)
        deg = jax.ops.segment_sum(jnp.ones((src.shape[0],), nodes.dtype), dst, num_segments=n)
        inv_deg = jnp.where(deg > 0, 1.0 / jnp.maximum(deg, 1.0), 0.0)[:, None]
        for i in range(DEPTH):
            msg = jnp.einsum('ei,eio->eo', nodes[src], w)
            agg = jax.ops.segment_sum(msg, dst, num_segments=n)
            agg = agg * inv_deg
            nodes = jax.nn.gelu(agg + nodes @ root_W[i] + root_b[i])
        return nodes
    edge_index = jnp.stack([src, dst])
    x = _layernorm(x + _L0_gnn_ref(x, edge_attr_6, L0_gnn_kW1, L0_gnn_kb1, L0_gnn_kW2, L0_gnn_kb2, L0_gnn_kW3, L0_gnn_kb3, L0_gnn_root_W, L0_gnn_root_b, edge_index), axis=-1)
    return x

_drawn_inputs = setup_inputs


def setup_inputs(seed=0):
    import zlib

    import numpy as np

    out = dict(_drawn_inputs(seed))
    spreads = {'L0_gnn_kb1': (0.0, 0.441),
     'L0_gnn_kb2': (0.0, 0.1),
     'L0_gnn_kb3': (0.0, 0.1),
     'L0_gnn_root_b': (0.0, 0.1)}
    factors = {'edge_attr_6': 3.918}
    for name, (base, spread) in spreads.items():
        noise = np.random.default_rng([zlib.crc32(name.encode()), seed]).standard_normal(out[name].shape)
        drawn = base * np.exp(spread * noise) if base else spread * noise
        out[name] = jnp.asarray(drawn.astype(out[name].dtype))
    for name, factor in factors.items():
        out[name] = (out[name] * factor).astype(out[name].dtype)
    return out
```

```python
import concourse.bass as bass
from concourse import mybir
from contextlib import ExitStack

P = 128
TPS = 4
SE = TPS * P
UNROLL = 8
HALF = UNROLL // 2
WIN = 32
WIDE = 512
CPG = 14
CPT = 7
LEAD = 4


def sizes(n_nodes, n_edges):
    chunks = -(-n_nodes // (P * CPG)) * CPG
    iters = -(-n_edges // (SE * UNROLL))
    return chunks, iters


def spread(ap, axis, n):
    shape = list(ap.shape)
    return ap.unsqueeze(axis).broadcast_to(shape[:axis] + [n] + shape[axis:])


def gnn_resnorm_kernel(nc, x_rows, attr_t, src_idx, dst_tiles, base_row, w1, b1, w2, b2, w3, b3,
                       root_w, root_b, out, n_edges):
    fp32, i32 = mybir.dt.float32, mybir.dt.int32
    ALU = mybir.AluOpType
    ACT = mybir.ActivationFunctionType
    AX = mybir.AxisListType

    L = 16
    EDIM, K = w1.shape
    DEPTH = root_w.shape[0]
    NB = x_rows.shape[1] // L
    NODES = P * NB
    NG = NB // CPG
    NT = NB // CPT
    TB = 4
    NTB = -(-NT // TB)
    NWIDE = -(-NODES // WIDE)
    TILES = dst_tiles.shape[1]
    SUPERS = TILES // TPS
    ITERS = SUPERS // UNROLL
    MX = 2 * L + 1
    MG = L + 1
    FULL, REST = n_edges // P, n_edges % P

    table = nc.dram_tensor("node_table", (NODES, L), fp32, kind="Internal").ap()
    table_rows = table.rearrange("(p c) i -> p (c i)", p=P)

    ctx = ExitStack()
    with ctx:
        def sb(name, shape, dt=fp32):
            return ctx.enter_context(nc.sbuf_tensor(name, shape, dt))

        def pb(name, shape):
            return ctx.enter_context(nc.psum_tensor(name, shape, fp32))

        def sem(name):
            return ctx.enter_context(nc.semaphore(name))

        w1_sb = sb("w1_sb", [EDIM, K])
        w2_sb = sb("w2_sb", [K, K])
        w3_sb = sb("w3_sb", [K, L * L])
        b1_sb = sb("b1_sb", [K, 1])
        b2_sb = sb("b2_sb", [K, 1])
        root_b_sb = sb("root_b_sb", [P, DEPTH, L])
        mix = sb("mix", [MX, MG])
        root_blocks = sb("root_blocks", [CPT * L, DEPTH, CPT * L])
        attr = sb("attr", [EDIM, 2, HALF * SE])
        idx = sb("idx", [P, 2, HALF * TPS], i32)
        h1 = sb("h1", [K, 2, SE])
        h2 = sb("h2", [K, 2, SE])
        prod = sb("prod", [P, 2, 2, L, L])
        mx = sb("mx", [P, HALF, TPS, MX])
        onehot = sb("onehot", [P, 2, TPS, WIN])
        shifted = sb("shifted", [P, TPS])
        wide_onehot = sb("wide_onehot", [P, TPS, WIDE])
        rel = sb("rel", [P, TILES])
        dst_f = sb("dst_f", [P, TILES])
        base_sb = sb("base_sb", [1, SUPERS], i32)
        agg = sb("agg", [MX, NWIDE * WIDE])
        rows = sb("rows", [P, NB, L])
        x_in = sb("x_in", [P, NB, L])
        rows_t = sb("rows_t", [CPT * L, NTB * TB, P])
        update = sb("update", [P, 2, CPG, L])
        mean_msg = sb("mean_msg", [P, CPG, L])
        inv_deg = sb("inv_deg", [P, 2, CPG])
        ident = sb("ident", [P, P])
        col_i = sb("col_i", [P, WIDE], i32)
        col_f = sb("col_f", [P, WIDE])
        row_i = sb("row_i", [P, 1], i32)
        row_f = sb("row_f", [P, 1])
        ones = sb("ones", [P, 1])
        eps = sb("eps", [P, 1])
        viol = sb("viol", [P, 2])
        viol_all = sb("viol_all", [P, 1])
        flag = sb("flag", [1, 1], i32)
        stat = sb("stat", [P, 4, NB])

        ps_h1 = pb("ps_h1", [P, SE])
        ps_h2 = pb("ps_h2", [P, SE])
        ps_w = pb("ps_w", [P, 4, 512])
        ps_win = pb("ps_win", [P, 2, 512])

        pool_turns = sem("pool_turns")
        pe_turns = sem("pe_turns")
        consts_in = sem("consts_in")
        zeroed = sem("zeroed")
        blocks_in = sem("blocks_in")
        dve_step = sem("dve_step")
        setup_dve = sem("setup_dve")
        flag_ps = sem("flag_ps")
        flag_set = sem("flag_set")
        attr_in = [sem(f"attr_in{h}") for h in range(2)]
        idx_in = [sem(f"idx_in{h}") for h in range(2)]
        x_in_sem = [sem(f"x_gathered{u}") for u in range(UNROLL)]
        h1_raw = sem("h1_raw")
        h1_done = sem("h1_done")
        h2_raw = sem("h2_raw")
        h2_done = sem("h2_done")
        w_done = sem("w_done")
        prod_done = sem("prod_done")
        msg_done = sem("msg_done")
        onehot_done = sem("onehot_done")
        win_done = sem("win_done")
        agg_done = sem("agg_done")
        wide_onehot_done = [sem(f"wide_onehot_done{u}") for u in range(UNROLL)]
        wide_win_done = [sem(f"wide_win_done{u}") for u in range(UNROLL)]
        wide_agg_done = [sem(f"wide_agg_done{u}") for u in range(UNROLL)]
        shift_done = [sem(f"shift_done{u}") for u in range(UNROLL)]
        transposed = sem("transposed")
        rows_t_done = sem("rows_t_done")
        update_raw = sem("update_raw")
        update_done = sem("update_done")
        rows_done = sem("rows_done")
        table_written = sem("table_written")
        var_done = sem("var_done")
        std_done = sem("std_done")
        normed = sem("normed")
        out_written = sem("out_written")

        NCONST = 10
        attr_chunk = attr_t.rearrange("e (c n) -> e c n", n=HALF * SE)
        dst_i = rel[:, :].bitcast(i32)
        base_all = sb("base_all", [P, SUPERS], i32)
        base_f = sb("base_f", [P, SUPERS])

        block = ctx.enter_context(nc.Block())

        @block.sync
        def _(sp):
            for dst, src in ((w1_sb[:, :], w1), (w2_sb[:, :], w2), (w3_sb[:, :], w3),
                             (b1_sb[:, :], b1), (b2_sb[:, :], b2),
                             (root_b_sb[:, :, :], root_b.rearrange("(o d) i -> o d i", o=1).broadcast_to([P, DEPTH, L])),
                             (dst_i, dst_tiles), (base_sb[:, :], base_row),
                             (base_all[:, :], base_row.broadcast_to([P, SUPERS])),
                             (x_in[:, :, :].rearrange("p c i -> p (c i)"), x_rows)):
                sp.dma_start(dst, src).then_inc(consts_in, 16)
            for h in range(2):
                sp.dma_start(attr[:, h, :], attr_chunk[:, h, :]).then_inc(attr_in[h], 16)
                sp.dma_start(idx[:, h, :], src_idx[h, :, :]).then_inc(idx_in[h], 16)
            sp.wait_ge(zeroed, 1)
            sp.dma_start(mix[L:2 * L, 0:L], b3).then_inc(blocks_in, 16)
            for b in range(CPT):
                sp.dma_start(root_blocks[b * L:(b + 1) * L, :, b * L:(b + 1) * L],
                             root_w.rearrange("d i o -> i d o")).then_inc(blocks_in, 16)
            with sp.Fori(0, DEPTH) as d:
                sp.wait_ge(rows_done, d * NG + NG)
                sp.dma_start(table_rows, rows[:, :, :].rearrange("p c i -> p (c i)")).then_inc(table_written, 16)
                with sp.Fori(0, ITERS) as it:
                    for h in range(2):
                        sp.wait_ge(h1_raw, (d * ITERS + it) * UNROLL + (LEAD + HALF * (h + 1)))
                        sp.dma_start(attr[:, h, :], attr_chunk[:, bass.ds(it * 2 + (2 + h), 1), :]
                                     .rearrange("e c n -> e (c n)")).then_inc(attr_in[h], 16)
                        for u in range(HALF * h, HALF * (h + 1)):
                            sp.wait_ge(x_in_sem[u], (d * ITERS + it) * (16 * TPS) + 16 * TPS)
                        sp.dma_start(idx[:, h, :], src_idx[bass.ds(it * 2 + (2 + h), 1), :, :]
                                     .rearrange("c p n -> (c p) n")).then_inc(idx_in[h], 16)
            for h in range(2):
                sp.wait_ge(attr_in[h], 16 * (DEPTH * ITERS + 1))
                sp.wait_ge(idx_in[h], 16 * (DEPTH * ITERS + 1))
            sp.wait_ge(normed, 1)
            sp.dma_start(out, x_in[:, :, :].rearrange("p c i -> p (c i)")).then_inc(out_written, 16)
            sp.wait_ge(table_written, 16 * DEPTH)
            sp.wait_ge(out_written, 16)

        @block.gpsimd
        def _(pool):
            nc.gpsimd.memset(mix[:, :], 0.0)
            nc.gpsimd.memset(root_blocks[:, :, :], 0.0).then_inc(zeroed, 1)
            nc.gpsimd.iota(col_i[:, :], pattern=[[1, WIDE]], base=0, channel_multiplier=0)
            nc.gpsimd.iota(row_i[:, :], pattern=[[1, 1]], base=0, channel_multiplier=1)
            nc.gpsimd.memset(mx[:, :, :, :], 1.0).then_inc(zeroed, 1)
            pool.wait_ge(zeroed, 2)
            with pool.Fori(0, DEPTH) as d:
                pool.wait_ge(table_written, d * 16 + 16)
                pool.sem_inc(pool_turns, 1)
                with pool.Fori(0, ITERS) as it:
                    for u in range(UNROLL):
                        if u % HALF == 0:
                            pool.wait_ge(idx_in[u // HALF], (d * ITERS + it) * 16 + 16)
                        pool.wait_ge(win_done, (d * ITERS + it) * UNROLL + (LEAD + u + 1 - HALF))
                        pool.sem_inc(pool_turns, 1)
                        for t in range(TPS):
                            c = (u % HALF) * TPS + t
                            nc.gpsimd.indirect_dma_start(
                                out=mx[:, u % HALF, t, L:2 * L], out_offset=None, in_=table,
                                in_offset=bass.IndirectOffsetOnAxis(ap=idx[:, u // HALF, c:c + 1], axis=0),
                            ).then_inc(x_in_sem[u], 16)

        @block.scalar
        def _(act):
            act.wait_ge(consts_in, 16 * NCONST)
            nc.scalar.copy(rows[:, :, :], x_in[:, :, :]).then_inc(rows_done, NG)

            def gelu1(g, slot, rings=True):
                act.wait_ge(h1_raw, g + (LEAD + 1))
                act.wait_ge(h2_raw, g + (LEAD - 1))
                nc.scalar.activation(h1[:, slot, :], ps_h1[:, :], ACT.Gelu_apprx_tanh,
                                     bias=b1_sb[:, 0:1]).then_inc(h1_done, 1)

            def gelu2(g, slot):
                act.wait_ge(h2_raw, g + (LEAD + 1))
                act.wait_ge(w_done, g * 2 + (LEAD - 2))
                nc.scalar.activation(h2[:, slot, :], ps_h2[:, :], ACT.Gelu_apprx_tanh,
                                     bias=b2_sb[:, 0:1]).then_inc(h2_done, 1)

            gelu1(0, 0)
            gelu1(1, 1)
            gelu2(0, 0)
            with act.Fori(0, DEPTH) as d:
                for k in range(NTB):
                    act.wait_ge(transposed, d * NTB + (k + 1))
                    n = min(TB, NT - TB * k)
                    nc.scalar.copy(rows_t[:, TB * k:TB * k + n, :],
                                   ps_win[0:CPT * L, k % 2, 0:n * P].rearrange("p (a b) -> p a b", b=P)
                                   ).then_inc(rows_t_done, 1)
                with act.Fori(0, ITERS) as it:
                    g0 = (d * ITERS + it) * UNROLL
                    for u in range(UNROLL):
                        gelu1(g0 + (u + 2), u % 2)
                        gelu2(g0 + (u + 1), (u + 1) % 2)
                for j in range(NG):
                    act.wait_ge(update_done, d * NG + (j + 1))
                    nc.scalar.activation(rows[:, CPG * j:CPG * (j + 1), :], update[:, j % 2, :, :],
                                         ACT.Gelu_apprx_tanh).then_inc(rows_done, 1)
            act.wait_ge(var_done, 1)
            nc.scalar.activation(stat[:, 2, :], stat[:, 1, :], ACT.Sqrt, bias=eps[:, 0:1],
                                 scale=1.0 / L).then_inc(std_done, 1)

        @block.vector
        def _(dve):
            steps = [0]

            def link(ins):
                steps[0] += 1
                ins.then_inc(dve_step, 1)
                dve.wait_ge(dve_step, steps[0])

            nc.vector.memset(agg[:, :], 0.0)
            nc.vector.memset(viol[:, :], 0.0)
            nc.vector.memset(eps[:, :], 1e-5)
            nc.vector.memset(ones[:, :], 1.0)
            dve.wait_ge(zeroed, 2)
            nc.vector.tensor_copy(col_f[:, :], col_i[:, :])
            link(nc.vector.tensor_copy(row_f[:, :], row_i[:, :]))
            link(nc.vector.tensor_scalar(ident[:, :], col_f[:, 0:P], row_f[:, 0:1], None, ALU.is_equal))
            dve.wait_ge(blocks_in, 16 * (1 + CPT))
            nc.vector.tensor_copy(mix[0:L, 0:L], ident[0:L, 0:L])
            link(nc.vector.memset(mix[2 * L:MX, L:MG], 1.0))
            dve.wait_ge(consts_in, 16 * NCONST)
            nc.vector.tensor_copy(base_f[:, :], base_all[:, :])
            link(nc.vector.tensor_copy(dst_f[:, :], dst_i))
            link(nc.vector.tensor_tensor(
                rel[:, :].rearrange("p (s t) -> p s t", t=TPS),
                dst_f[:, :].rearrange("p (s t) -> p s t", t=TPS),
                spread(base_f[:, :], 2, TPS), ALU.subtract))
            for n, (q, a, b) in enumerate(((P, 0, FULL), (REST, FULL, FULL + 1))):
                if q == 0 or a == b:
                    continue
                for lo in range(a, b, WIDE * TPS):
                    hi = min(lo + WIDE * TPS, b)
                    tmp = wide_onehot[:, :, :].rearrange("p t w -> p (t w)")[0:q, 0:hi - lo]
                    link(nc.vector.tensor_scalar(tmp, rel[0:q, lo:hi], 0.0, float(WIN - 1), ALU.max, ALU.min))
                    link(nc.vector.tensor_tensor(tmp, tmp, rel[0:q, lo:hi], ALU.not_equal))
                    link(nc.vector.tensor_reduce(viol[0:q, 1:2], tmp, AX.X, ALU.add))
                    link(nc.vector.tensor_tensor(viol[0:q, 0:1], viol[0:q, 0:1], viol[0:q, 1:2], ALU.add))
            nc.vector.tensor_copy(viol_all[:, :], viol[:, 0:1]).then_inc(setup_dve, 1)
            dve.wait_ge(flag_ps, 1)
            link(nc.vector.tensor_copy(flag[0:1, 0:1], ps_win[0:1, 0, 0:1]))
            n_setup = steps[0]
            dve.sem_inc(flag_set, 1)
            is_wide = dve.value_load(flag[0:1, 0:1], min_val=0, max_val=1 << 20)

            def super_tile(d, it, u, wide):
                slot = u % HALF
                itg = d * ITERS + it
                g = itg * UNROLL + u
                if not wide:
                    dve.wait_ge(win_done, g + (LEAD - 1))
                    nc.vector.tensor_tensor(
                        onehot[:, u % 2, :, :], spread(col_f[:, 0:WIN], 1, TPS),
                        spread(rel[:, bass.ds((it * UNROLL + u) * TPS, TPS)], 2, WIN),
                        ALU.is_equal).then_inc(onehot_done, 1)
                dve.wait_ge(x_in_sem[u], itg * (16 * TPS) + 16 * TPS)
                for h in range(2):
                    dve.wait_ge(w_done, g * 2 + (LEAD + h + 1))
                    dve.wait_ge(msg_done, g * 2 + (LEAD + h - 1))
                    nc.vector.tensor_tensor(
                        prod[:, h, :, :, :],
                        ps_w[:, (2 * u + h) % 4, :].rearrange("p (t o i) -> p t o i", t=2, o=L),
                        spread(mx[:, slot, 2 * h:2 * h + 2, L:2 * L], 2, L),
                        ALU.mult).then_inc(prod_done, 1)
                for h in range(2):
                    dve.wait_ge(prod_done, g * 2 + (LEAD + h + 1))
                    nc.vector.tensor_reduce(mx[:, slot, 2 * h:2 * h + 2, 0:L], prod[:, h, :, :, :],
                                            AX.X, ALU.add).then_inc(msg_done, 1)

            def add_window(d, it, u):
                g = (d * ITERS + it) * UNROLL + u
                base = dve.value_load(base_sb[0:1, bass.ds(it * UNROLL + u, 1)], min_val=0,
                                      max_val=NODES - WIN)
                dve.wait_ge(win_done, g + (LEAD + 1))
                dve.wait_ge(agg_done, g + LEAD)
                nc.vector.tensor_tensor(agg[:, bass.ds(base, WIN)], agg[:, bass.ds(base, WIN)],
                                        ps_win[0:MX, u % 2, 0:WIN], ALU.add).then_inc(agg_done, 1)

            def add_wide(d, it, u):
                itg = d * ITERS + it
                nc.vector.tensor_copy(shifted[:, :], dst_f[:, bass.ds((it * UNROLL + u) * TPS, TPS)]
                                      ).then_inc(shift_done[u], 1)
                with dve.Fori(0, NWIDE) as j:
                    n = itg * NWIDE + j
                    dve.wait_ge(shift_done[u], itg * (NWIDE + 1) + j + 1)
                    nc.vector.tensor_tensor(wide_onehot[:, :, :], spread(col_f[:, :], 1, TPS),
                                            spread(shifted[:, :], 2, WIDE),
                                            ALU.is_equal).then_inc(wide_onehot_done[u], 1)
                    dve.wait_ge(wide_win_done[u], n + 1)
                    nc.vector.tensor_tensor(agg[:, bass.ds(j * WIDE, WIDE)], agg[:, bass.ds(j * WIDE, WIDE)],
                                            ps_win[0:MX, u % 2, :], ALU.add).then_inc(wide_agg_done[u], 1)
                    dve.wait_ge(wide_onehot_done[u], n + 1)
                    dve.wait_ge(wide_agg_done[u], n + 1)
                    nc.vector.tensor_scalar(shifted[:, :], shifted[:, :], -float(WIDE), None,
                                            ALU.add).then_inc(shift_done[u], 1)
                dve.wait_ge(shift_done[u], itg * (NWIDE + 1) + (NWIDE + 1))
                dve.sem_inc(agg_done, 1)

            def depth_end(d):
                for j in range(NG):
                    acc = ps_w[:, j % 4, 0:CPG * MG].rearrange("p (c m) -> p c m", m=MG)
                    root = ps_w[:, j % 4, CPG * MG:CPG * (MG + L)].rearrange("p (c m) -> p c m", m=L)
                    dve.wait_ge(update_raw, d * NG + (j + 1))
                    k = d * (5 * NG) + (n_setup + 5 * j)
                    nc.vector.tensor_scalar(inv_deg[:, 0, :], acc[:, :, L:MG].rearrange("p c o -> p (c o)"),
                                            1.0, None, ALU.max).then_inc(dve_step, 1)
                    dve.wait_ge(dve_step, k + 1)
                    nc.vector.reciprocal(inv_deg[:, 1, :], inv_deg[:, 0, :]).then_inc(dve_step, 1)
                    dve.wait_ge(dve_step, k + 2)
                    nc.vector.tensor_tensor(mean_msg[:, :, :], acc[:, :, 0:L],
                                            spread(inv_deg[:, 1, :], 2, L),
                                            ALU.mult).then_inc(dve_step, 1)
                    dve.wait_ge(dve_step, k + 3)
                    nc.vector.tensor_tensor(mean_msg[:, :, :], mean_msg[:, :, :], root, ALU.add).then_inc(dve_step, 1)
                    dve.wait_ge(dve_step, k + 4)
                    dve.wait_ge(rows_done, d * NG + (NG + j - 1))
                    nc.vector.tensor_tensor(update[:, j % 2, :, :], mean_msg[:, :, :],
                                            root_b_sb[:, bass.ds(d, 1), :].broadcast_to([P, CPG, L]),
                                            ALU.add).then_inc(update_done, 1)
                    dve.wait_ge(update_done, d * NG + (j + 1))
                    dve.sem_inc(dve_step, 1)
                nc.vector.memset(agg[:, :], 0.0)

            with dve.Fori(0, DEPTH) as d:
                with dve.If(is_wide > 0):
                    with dve.Fori(0, ITERS) as it:
                        for u in range(UNROLL):
                            super_tile(d, it, u, True)
                            add_wide(d, it, u)
                with dve.Else():
                    with dve.Fori(0, ITERS) as it:
                        for u in range(UNROLL):
                            super_tile(d, it, u, False)
                            if u:
                                add_window(d, it, u - 1)
                        add_window(d, it, UNROLL - 1)
                depth_end(d)

            dve.wait_ge(rows_done, (DEPTH + 1) * NG)
            steps[0] = n_setup + 5 * NG * DEPTH
            link(nc.vector.tensor_tensor(rows[:, :, :], rows[:, :, :], x_in[:, :, :], ALU.add))
            link(nc.vector.tensor_reduce(stat[:, 0, :], rows[:, :, :], AX.X, ALU.add))
            link(nc.vector.tensor_scalar(stat[:, 0, :], stat[:, 0, :], 1.0 / L, None, ALU.mult))
            link(nc.vector.tensor_tensor(rows[:, :, :], rows[:, :, :],
                                         spread(stat[:, 0, :], 2, L), ALU.subtract))
            link(nc.vector.tensor_tensor(x_in[:, :, :], rows[:, :, :], rows[:, :, :], ALU.mult))
            nc.vector.tensor_reduce(stat[:, 1, :], x_in[:, :, :], AX.X, ALU.add).then_inc(var_done, 1)
            dve.wait_ge(std_done, 1)
            link(nc.vector.reciprocal(stat[:, 3, :], stat[:, 2, :]))
            nc.vector.tensor_tensor(x_in[:, :, :], rows[:, :, :],
                                    spread(stat[:, 3, :], 2, L), ALU.mult).then_inc(normed, 1)

        @block.tensor
        def _(pe):
            def layer1(g, s, first=False):
                if s % HALF == 0 or first:
                    pe.wait_ge(attr_in[s // HALF % 2], first if first else (g[1] * 16 + 16 * (1 + s // UNROLL)))
                pe.wait_ge(h1_done, g[0] + (LEAD + s))
                nc.tensor.matmul(ps_h1[:, :], w1_sb[:, :], attr[:, s // HALF % 2, s % HALF * SE:(s % HALF + 1) * SE],
                                 start=True, stop=True).then_inc(h1_raw, 1)

            def layer2(g, s):
                pe.wait_ge(h1_done, g[0] + (LEAD + s + 1))
                pe.wait_ge(h2_done, g[0] + (LEAD + s))
                nc.tensor.matmul(ps_h2[:, :], w2_sb[:, :], h1[:, s % 2, :], start=True, stop=True).then_inc(h2_raw, 1)

            def layer3(g, s, h):
                if h == 0:
                    pe.wait_ge(h2_done, g[0] + (LEAD + s + 1))
                pe.wait_ge(prod_done, g[0] * 2 + (LEAD + 2 * s + h - 3))
                for t in range(2):
                    last = nc.tensor.matmul(ps_w[:, (2 * s + h) % 4, t * L * L:(t + 1) * L * L],
                                            h2[:, s % 2, (2 * h + t) * P:(2 * h + t + 1) * P], w3_sb[:, :],
                                            start=True, stop=True)
                last.then_inc(w_done, 1)

            def scatter(g, s):
                pe.wait_ge(msg_done, g[0] * 2 + (LEAD + 2 * s + 2))
                pe.wait_ge(onehot_done, g[0] + (LEAD + s + 1))
                pe.wait_ge(agg_done, g[0] + (LEAD + s - 1))
                for t in range(TPS):
                    last = nc.tensor.matmul(ps_win[0:MX, s % 2, 0:WIN], mx[:, s % HALF, t, :],
                                            onehot[:, s % 2, t, :], start=(t == 0), stop=(t == TPS - 1))
                last.then_inc(win_done, 1)

            def scatter_wide(g, s):
                pe.wait_ge(msg_done, g[0] * 2 + (LEAD + 2 * s + 2))
                pe.sem_inc(pe_turns, 1)
                with pe.Fori(0, NWIDE) as j:
                    pe.wait_ge(wide_onehot_done[s], g[1] * NWIDE + j + 1)
                    for t in range(TPS):
                        last = nc.tensor.matmul(ps_win[0:MX, s % 2, :], mx[:, s % HALF, t, :],
                                                wide_onehot[:, t, :], start=(t == 0), stop=(t == TPS - 1))
                    last.then_inc(wide_win_done[s], 1)
                pe.wait_ge(wide_agg_done[s], g[1] * NWIDE + NWIDE)
                pe.sem_inc(win_done, 1)

            pe.wait_ge(setup_dve, 1)
            nc.tensor.matmul(ps_win[0:1, 0, 0:1], viol_all[:, :], ones[:, :], start=True, stop=True).then_inc(flag_ps, 1)
            for s in (h1_raw, h1_done, h2_raw, h2_done, w_done, prod_done, msg_done, onehot_done, win_done, agg_done):
                pe.sem_inc(s, LEAD)
            pe.wait_ge(flag_set, 1)
            is_wide = pe.value_load(flag[0:1, 0:1], min_val=0, max_val=1 << 20)
            pe.wait_ge(attr_in[0], 16)
            layer1((0, 0), 0, first=16)
            layer1((0, 0), 1)
            layer2((0, 0), 0)
            with pe.Fori(0, DEPTH) as d:
                pe.wait_ge(rows_done, d * NG + NG)
                for k in range(NTB):
                    if k >= 2:
                        pe.wait_ge(rows_t_done, d * NTB + (k - 1))
                    for a in range(TB * k, min(TB * (k + 1), NT)):
                        last = nc.tensor.transpose(
                            ps_win[0:CPT * L, k % 2, (a % TB) * P:(a % TB + 1) * P],
                            rows[:, CPT * a:CPT * (a + 1), :].rearrange("p c i -> p (c i)"), ident[:, :])
                    last.then_inc(transposed, 1)
                pe.wait_ge(rows_t_done, d * NTB + NTB)
                pe.sem_inc(pe_turns, 1)
                with pe.If(is_wide > 0):
                    with pe.Fori(0, ITERS) as it:
                        g = ((d * ITERS + it) * UNROLL, d * ITERS + it)
                        for u in range(UNROLL):
                            layer3(g, u, 0)
                            layer3(g, u, 1)
                            layer1(g, u + 2)
                            layer2(g, u + 1)
                            scatter_wide(g, u)
                with pe.Else():
                    with pe.Fori(0, ITERS) as it:
                        g = ((d * ITERS + it) * UNROLL, d * ITERS + it)
                        for u in range(UNROLL):
                            layer3(g, u, 0)
                            if u:
                                scatter(g, u - 1)
                            layer3(g, u, 1)
                            layer1(g, u + 2)
                            layer2(g, u + 1)
                        scatter(g, UNROLL - 1)
                pe.wait_ge(agg_done, d * SUPERS + (LEAD + SUPERS))
                for j in range(NG):
                    if j >= 4:
                        pe.wait_ge(update_done, d * NG + (j - 3))
                    for c in range(CPG):
                        nc.tensor.matmul(ps_w[:, j % 4, c * MG:(c + 1) * MG],
                                         agg[:, bass.ds(CPG * j + c, P, step=NB)], mix[:, :],
                                         start=True, stop=True)
                    for r in range(CPG // CPT):
                        at = CPG * MG + r * CPT * L
                        last = nc.tensor.matmul(ps_w[:, j % 4, at:at + CPT * L],
                                                rows_t[:, (CPG // CPT) * j + r, :],
                                                root_blocks[:, bass.ds(d, 1), :].rearrange("p d n -> p (d n)"),
                                                start=True, stop=True)
                    last.then_inc(update_raw, 1)


def kernel(x, src, dst, edge_attr_6, L0_gnn_kW1, L0_gnn_kb1, L0_gnn_kW2, L0_gnn_kb2, L0_gnn_kW3, L0_gnn_kb3,
           L0_gnn_root_W, L0_gnn_root_b):
    import numpy as np
    import concourse.bacc as bacc
    from concourse import mybir
    from concourse.bass_utils import run_bass_kernel_spmd

    x, src, dst, edge_attr = (np.asarray(a) for a in (x, src, dst, edge_attr_6))
    n, l = x.shape
    e = src.shape[0]
    nb, iters = sizes(n, e)
    slots = iters * UNROLL * SE
    extra = 2 * HALF * SE

    x_rows = np.zeros((P * nb, l), x.dtype)
    x_rows[:n] = x
    attr_t = np.zeros((edge_attr.shape[1], slots + extra), edge_attr.dtype)
    attr_t[:, :e] = edge_attr.T
    attr_t[:, slots:] = attr_t[:, :extra]
    src_pad = np.zeros(slots + extra, src.dtype)
    src_pad[:e] = src
    src_pad[slots:] = src_pad[:extra]
    src_idx = src_pad.reshape(-1, HALF * TPS, P).transpose(0, 2, 1)
    dst_pad = np.full(slots, -1, dst.dtype)
    dst_pad[:e] = dst
    dst_tiles = dst_pad.reshape(-1, P).T
    base_row = np.zeros((1, slots // SE), dst.dtype)
    first = dst_pad[::SE]
    used = -(-e // SE)
    base_row[0, :used] = first[:used]
    w3 = np.asarray(L0_gnn_kW3).reshape(-1, l, l).transpose(0, 2, 1).reshape(-1, l * l)
    arrays = dict(
        x_rows=x_rows.reshape(P, nb * l), attr_t=attr_t, src_idx=src_idx, dst_tiles=dst_tiles, base_row=base_row,
        w1=L0_gnn_kW1, b1=np.asarray(L0_gnn_kb1).reshape(-1, 1), w2=L0_gnn_kW2,
        b2=np.asarray(L0_gnn_kb2).reshape(-1, 1), w3=w3, b3=np.asarray(L0_gnn_kb3).reshape(l, l),
        root_w=L0_gnn_root_W, root_b=L0_gnn_root_b)
    arrays = {k: np.ascontiguousarray(v) for k, v in arrays.items()}

    nc = bacc.Bacc("TRN2", target_bir_lowering=False, num_devices=1)
    ins = {k: nc.dram_tensor(k, v.shape, mybir.dt.from_np(v.dtype), kind="ExternalInput").ap()
           for k, v in arrays.items()}
    out = nc.dram_tensor("out", (P, nb * l), mybir.dt.float32, kind="ExternalOutput").ap()
    gnn_resnorm_kernel(nc, **ins, out=out, n_edges=e)
    r = run_bass_kernel_spmd(nc, [arrays], core_ids=[0])
    return r.results[0]["out"].reshape(P * nb, l)[:n]
```

```python
import concourse.bass as bass
from concourse import mybir
from contextlib import ExitStack

P = 128
TPS = 4
SE = TPS * P
UNROLL = 8
HALF = UNROLL // 2
WIN = 32
WIDE = 512
CPG = 14
CPT = 7
LEAD = 1


def sizes(n_nodes, n_edges):
    chunks = -(-n_nodes // (P * CPG)) * CPG
    iters = -(-n_edges // (SE * UNROLL))
    return chunks, iters


def spread(ap, axis, n):
    shape = list(ap.shape)
    return ap.unsqueeze(axis).broadcast_to(shape[:axis] + [n] + shape[axis:])


def gnn_resnorm_kernel(nc, x_rows, attr_in, src_idx, dst_tiles, base_row, w1, b1, w2, b2, w3, b3,
                       root_w, root_b, out, n_edges):
    fp32, i32, bf16 = mybir.dt.float32, mybir.dt.int32, mybir.dt.bfloat16
    ALU = mybir.AluOpType
    ACT = mybir.ActivationFunctionType
    AX = mybir.AxisListType

    L = 16
    EDIM, K = w1.shape
    DEPTH = root_w.shape[0]
    NB = x_rows.shape[1] // L
    NODES = P * NB
    NG = NB // CPG
    NT = NB // CPT
    TB = 4
    NTB = -(-NT // TB)
    NWIDE = -(-NODES // WIDE)
    TILES = dst_tiles.shape[1]
    SUPERS = TILES // TPS
    ITERS = SUPERS // UNROLL
    MX = 2 * L + 1
    MG = L + 1
    FULL, REST = n_edges // P, n_edges % P

    table = nc.dram_tensor("node_table", (NODES, L), fp32, kind="Internal").ap()
    PASSES = attr_in.shape[0]
    PASS_E = UNROLL * SE
    SEG = 16
    SEGW = PASS_E // SEG
    SPLIT = max(k for k in range(1, 7) if PASSES % k == 0)
    NSPLIT = PASSES // SPLIT
    W1R = 2 * 32 + 3 * EDIM
    attr_parts = nc.dram_tensor("attr_parts", (PASSES, 3 * EDIM, PASS_E), bf16, kind="Internal").ap()
    table_rows = table.rearrange("(p c) i -> p (c i)", p=P)

    ctx = ExitStack()
    with ctx:
        def sb(name, shape, dt=fp32):
            return ctx.enter_context(nc.sbuf_tensor(name, shape, dt))

        def pb(name, shape):
            return ctx.enter_context(nc.psum_tensor(name, shape, fp32))

        def sem(name):
            return ctx.enter_context(nc.semaphore(name))

        w1_rows = sb("w1_rows", [W1R, K])
        w1_rest = sb("w1_rest", [W1R, K])
        w1_parts = sb("w1_parts", [W1R, 3, K], bf16)
        w1_sb = sb("w1_sb", [W1R, K], bf16)
        w2_sb = sb("w2_sb", [K, K])
        w3_sb = sb("w3_sb", [K, L * L])
        b1_sb = sb("b1_sb", [K, 1])
        b2_sb = sb("b2_sb", [K, 1])
        root_b_sb = sb("root_b_sb", [P, DEPTH, L])
        mix = sb("mix", [MX, MG])
        root_blocks = sb("root_blocks", [CPT * L, DEPTH, CPT * L])
        attr = sb("attr", [W1R, 2, HALF * SE], bf16)
        split_parts = sb("split_parts", [EDIM * SEG, 2, 3, SPLIT * SEGW], bf16)
        idx = sb("idx", [P, 2, HALF * TPS], i32)
        h1 = sb("h1", [K, 2, SE])
        h2 = sb("h2", [K, 2, SE])
        prod = sb("prod", [P, 4, 2, L, L])
        mx = sb("mx", [P, UNROLL, TPS, MX])
        onehot = sb("onehot", [P, 2, HALF * TPS, WIN])
        shifted = sb("shifted", [P, TPS])
        wide_onehot = sb("wide_onehot", [P, TPS, WIDE])
        rel = sb("rel", [P, TILES])
        dst_f = sb("dst_f", [P, TILES])
        base_sb = sb("base_sb", [1, SUPERS], i32)
        agg_all = sb("agg_all", [P, NWIDE * WIDE])
        agg = agg_all[0:MX, :]
        split_in = [agg_all[0:EDIM * SEG, k * SPLIT * SEGW:(k + 1) * SPLIT * SEGW] for k in range(2)]
        split_rest = [agg_all[0:EDIM * SEG, (2 + k) * SPLIT * SEGW:(3 + k) * SPLIT * SEGW] for k in range(2)]
        rows = sb("rows", [P, NB, L])
        x_in = sb("x_in", [P, NB, L])
        rows_t = sb("rows_t", [CPT * L, NTB * TB, P])
        update = sb("update", [P, 2, CPG, L])
        mean_msg = sb("mean_msg", [P, CPG, L])
        inv_deg = sb("inv_deg", [P, 2, CPG])
        ident = sb("ident", [P, P])
        col_i = sb("col_i", [P, WIDE], i32)
        col_f = sb("col_f", [P, WIDE])
        row_i = sb("row_i", [P, 1], i32)
        row_f = sb("row_f", [P, 1])
        ones = sb("ones", [P, 1])
        eps = sb("eps", [P, 1])
        viol = sb("viol", [P, 2])
        viol_all = sb("viol_all", [P, 1])
        flag = sb("flag", [1, 1], i32)
        stat = sb("stat", [P, 4, NB])

        ps_h1 = pb("ps_h1", [P, SE])
        ps_h2 = pb("ps_h2", [P, SE])
        ps_w = pb("ps_w", [P, 4, 512])
        ps_win = pb("ps_win", [P, 2, 512])

        pool_turns = sem("pool_turns")
        pe_turns = sem("pe_turns")
        consts_in = sem("consts_in")
        zeroed = sem("zeroed")
        blocks_in = sem("blocks_in")
        dve_step = sem("dve_step")
        setup_dve = sem("setup_dve")
        flag_ps = sem("flag_ps")
        flag_set = sem("flag_set")
        attr_landed = [sem(f"attr_landed{h}") for h in range(2)]
        split_loaded = [sem(f"split_loaded{k}") for k in range(2)]
        split_written = [sem(f"split_written{k}") for k in range(2)]
        part1_done = sem("part1_done")
        rest_done = sem("rest_done")
        part2_done = sem("part2_done")
        part3_done = sem("part3_done")
        w1_done = sem("w1_done")
        idx_in = [sem(f"idx_in{h}") for h in range(2)]
        x_in_sem = [sem(f"x_gathered{u}") for u in range(UNROLL)]
        h1_raw = [sem(f"h1_raw{u}") for u in range(UNROLL)]
        h1_done = [sem(f"h1_done{u}") for u in range(UNROLL)]
        h2_raw = [sem(f"h2_raw{u}") for u in range(UNROLL)]
        h2_done = [sem(f"h2_done{u}") for u in range(UNROLL)]
        w_done = [sem(f"w_done{q}") for q in range(2 * UNROLL)]
        prod_done = [sem(f"prod_done{q}") for q in range(2 * UNROLL)]
        msg_done = [sem(f"msg_done{u}") for u in range(UNROLL)]
        onehot_done = [sem(f"onehot_done{h}") for h in range(2)]
        win_done = [sem(f"win_done{u}") for u in range(UNROLL)]
        agg_done = [sem(f"agg_done{u}") for u in range(UNROLL)]
        wide_onehot_done = [sem(f"wide_onehot_done{u}") for u in range(HALF)]
        wide_win_done = [sem(f"wide_win_done{u}") for u in range(HALF)]
        wide_agg_done = [sem(f"wide_agg_done{u}") for u in range(HALF)]
        shift_done = [sem(f"shift_done{u}") for u in range(HALF)]
        transposed = sem("transposed")
        rows_t_done = sem("rows_t_done")
        update_raw = sem("update_raw")
        update_done = sem("update_done")
        rows_done = sem("rows_done")
        table_written = sem("table_written")
        var_done = sem("var_done")
        std_done = sem("std_done")
        normed = sem("normed")
        out_written = sem("out_written")

        NCONST = 18

        def pass_values(eng, d, it):
            n = d * ITERS + it
            return {k: eng.snap(n + (LEAD + 1 + k)) for k in (-1, 0, 1)}

        def step_done(eng, sems, s, passes):
            eng.wait_ge(sems[s % UNROLL], passes[s // UNROLL])

        def half_done(eng, sems, s, h, passes):
            eng.wait_ge(sems[2 * (s % UNROLL) + h], passes[s // UNROLL])
        dst_i = rel[:, :].bitcast(i32)
        base_all = sb("base_all", [P, SUPERS], i32)
        base_f = sb("base_f", [P, SUPERS])

        block = ctx.enter_context(nc.Block())

        @block.sync
        def _(sp):
            def split_load(n):
                sp.dma_start(split_in[n % 2].rearrange("p (q w) -> p q w", w=SEGW),
                             attr_in[n * SPLIT:(n + 1) * SPLIT, :, :].rearrange("q e (s w) -> (e s) q w", w=SEGW)
                             ).then_inc(split_loaded[n % 2], 16)

            def attr_load(h, at):
                for j in range(3):
                    sp.dma_start(attr[32 * j:32 * j + 3 * EDIM, h, :],
                                 attr_parts[at, :, h * HALF * SE:(h + 1) * HALF * SE]
                                 ).then_inc(attr_landed[h], 16)

            split_load(0)
            split_load(1)
            sp.wait_ge(zeroed, 2)
            for b in range(3):
                for i in range(3):
                    at = 32 * b + i * EDIM
                    sp.dma_start(w1_rows[at:at + EDIM, :], w1).then_inc(consts_in, 16)
            for dst, src in ((w2_sb[:, :], w2), (w3_sb[:, :], w3),
                             (b1_sb[:, :], b1), (b2_sb[:, :], b2),
                             (root_b_sb[:, :, :], root_b.rearrange("(o d) i -> o d i", o=1).broadcast_to([P, DEPTH, L])),
                             (dst_i, dst_tiles), (base_sb[:, :], base_row),
                             (base_all[:, :], base_row.broadcast_to([P, SUPERS])),
                             (x_in[:, :, :].rearrange("p c i -> p (c i)"), x_rows)):
                sp.dma_start(dst, src).then_inc(consts_in, 16)
            for h in range(2):
                sp.dma_start(idx[:, h, :], src_idx[h, :, :]).then_inc(idx_in[h], 16)
            sp.wait_ge(zeroed, 1)
            sp.dma_start(mix[L:2 * L, 0:L], b3).then_inc(blocks_in, 16)
            for b in range(CPT):
                sp.dma_start(root_blocks[b * L:(b + 1) * L, :, b * L:(b + 1) * L],
                             root_w.rearrange("d i o -> i d o")).then_inc(blocks_in, 16)
            for n in range(NSPLIT):
                sp.wait_ge(part3_done, n + 1)
                for i in range(3):
                    sp.dma_start(attr_parts[n * SPLIT:(n + 1) * SPLIT, i * EDIM:(i + 1) * EDIM, :]
                                 .rearrange("q e (s w) -> (e s) q w", w=SEGW),
                                 split_parts[:, n % 2, i, :].rearrange("p (q w) -> p q w", w=SEGW)
                                 ).then_inc(split_written[n % 2], 16)
                if n + 2 < NSPLIT:
                    split_load(n + 2)
                if n == 0:
                    sp.wait_ge(split_written[0], 48)
                    sp.wait_ge(zeroed, 2)
                    attr_load(0, 0)
                    attr_load(1, 0)
            for k in range(2):
                sp.wait_ge(split_written[k], 48 * ((NSPLIT + 1 - k) // 2))
            with sp.Fori(0, DEPTH) as d:
                sp.wait_ge(rows_done, d * NG + NG)
                sp.dma_start(table_rows, rows[:, :, :].rearrange("p c i -> p (c i)")).then_inc(table_written, 16)
                with sp.Fori(0, ITERS) as it:
                    passes = pass_values(sp, d, it)
                    for h in range(2):
                        step_done(sp, h1_raw, HALF * (h + 1) - 1, passes)
                        for j in range(3):
                            sp.dma_start(attr[32 * j:32 * j + 3 * EDIM, h, :],
                                         attr_parts[bass.ds(it + 1, 1), :, h * HALF * SE:(h + 1) * HALF * SE]
                                         .rearrange("q r n -> (q r) n")).then_inc(attr_landed[h], 16)
                        for u in range(HALF * h, HALF * (h + 1)):
                            sp.wait_ge(x_in_sem[u], (d * ITERS + it) * (16 * TPS) + 16 * TPS)
                        sp.dma_start(idx[:, h, :], src_idx[bass.ds(it * 2 + (2 + h), 1), :, :]
                                     .rearrange("c p n -> (c p) n")).then_inc(idx_in[h], 16)
            for h in range(2):
                sp.wait_ge(attr_landed[h], 48 * (DEPTH * ITERS + 1))
                sp.wait_ge(idx_in[h], 16 * (DEPTH * ITERS + 1))
            sp.wait_ge(normed, 1)
            sp.dma_start(out, x_in[:, :, :].rearrange("p c i -> p (c i)")).then_inc(out_written, 16)
            sp.wait_ge(table_written, 16 * DEPTH)
            sp.wait_ge(out_written, 16)

        @block.gpsimd
        def _(pool):
            nc.gpsimd.memset(mix[:, :], 0.0)
            nc.gpsimd.memset(root_blocks[:, :, :], 0.0).then_inc(zeroed, 1)
            nc.gpsimd.iota(col_i[:, :], pattern=[[1, WIDE]], base=0, channel_multiplier=0)
            nc.gpsimd.iota(row_i[:, :], pattern=[[1, 1]], base=0, channel_multiplier=1)
            nc.gpsimd.memset(attr[:, :, :], 0.0)
            nc.gpsimd.memset(w1_rows[:, :], 0.0)
            nc.gpsimd.memset(mx[:, :, :, :], 1.0).then_inc(zeroed, 1)
            pool.wait_ge(zeroed, 2)
            with pool.Fori(0, DEPTH) as d:
                pool.wait_ge(table_written, d * 16 + 16)
                pool.sem_inc(pool_turns, 1)
                with pool.Fori(0, ITERS) as it:
                    passes = pass_values(pool, d, it)
                    for u in range(UNROLL):
                        if u % HALF == 0:
                            pool.wait_ge(idx_in[u // HALF], (d * ITERS + it) * 16 + 16)
                        step_done(pool, win_done, u - UNROLL, passes)
                        pool.sem_inc(pool_turns, 1)
                        for t in range(TPS):
                            c = (u % HALF) * TPS + t
                            nc.gpsimd.indirect_dma_start(
                                out=mx[:, u, t, L:2 * L], out_offset=None, in_=table,
                                in_offset=bass.IndirectOffsetOnAxis(ap=idx[:, u // HALF, c:c + 1], axis=0),
                            ).then_inc(x_in_sem[u], 16)

        @block.scalar
        def _(act):
            for n in range(NSPLIT + 1):
                if n < NSPLIT:
                    act.wait_ge(split_loaded[n % 2], 16 * (n // 2 + 1))
                    if n >= 2:
                        act.wait_ge(split_written[n % 2], 48 * (n // 2))
                    nc.scalar.copy(split_parts[:, n % 2, 0, :], split_in[n % 2]).then_inc(part1_done, 1)
                if n >= 1:
                    act.wait_ge(rest_done, n)
                    nc.scalar.copy(split_parts[:, (n - 1) % 2, 1, :], split_rest[(n - 1) % 2]).then_inc(part2_done, 1)
            act.wait_ge(consts_in, 16 * NCONST)
            nc.scalar.copy(rows[:, :, :], x_in[:, :, :]).then_inc(rows_done, NG)

            first = {-1: LEAD, 0: LEAD + 1}

            def gelu1(s, passes):
                step_done(act, h1_raw, s, passes)
                step_done(act, h2_raw, s - 2, passes)
                nc.scalar.activation(h1[:, s % 2, :], ps_h1[:, :], ACT.Gelu_apprx_tanh,
                                     bias=b1_sb[:, 0:1]).then_inc(h1_done[s % UNROLL], 1)

            def gelu2(s, passes):
                step_done(act, h2_raw, s, passes)
                half_done(act, w_done, s - 2, 1, passes)
                nc.scalar.activation(h2[:, s % 2, :], ps_h2[:, :], ACT.Gelu_apprx_tanh,
                                     bias=b2_sb[:, 0:1]).then_inc(h2_done[s % UNROLL], 1)

            gelu1(0, first)
            gelu1(1, first)
            gelu2(0, first)
            with act.Fori(0, DEPTH) as d:
                for k in range(NTB):
                    act.wait_ge(transposed, d * NTB + (k + 1))
                    n = min(TB, NT - TB * k)
                    nc.scalar.copy(rows_t[:, TB * k:TB * k + n, :],
                                   ps_win[0:CPT * L, k % 2, 0:n * P].rearrange("p (a b) -> p a b", b=P)
                                   ).then_inc(rows_t_done, 1)
                with act.Fori(0, ITERS) as it:
                    passes = pass_values(act, d, it)
                    for u in range(UNROLL):
                        gelu2(u + 1, passes)
                        gelu1(u + 2, passes)
                for j in range(NG):
                    act.wait_ge(update_done, d * NG + (j + 1))
                    nc.scalar.activation(rows[:, CPG * j:CPG * (j + 1), :], update[:, j % 2, :, :],
                                         ACT.Gelu_apprx_tanh).then_inc(rows_done, 1)
            act.wait_ge(var_done, 1)
            nc.scalar.activation(stat[:, 2, :], stat[:, 1, :], ACT.Sqrt, bias=eps[:, 0:1],
                                 scale=1.0 / L).then_inc(std_done, 1)

        @block.vector
        def _(dve):
            steps = [0]

            def link(ins):
                steps[0] += 1
                ins.then_inc(dve_step, 1)
                dve.wait_ge(dve_step, steps[0])

            for n in range(NSPLIT + 1):
                if n < NSPLIT:
                    dve.wait_ge(part1_done, n + 1)
                    nc.vector.tensor_tensor(split_rest[n % 2], split_in[n % 2], split_parts[:, n % 2, 0, :],
                                            ALU.subtract).then_inc(rest_done, 1)
                if n >= 1:
                    dve.wait_ge(part2_done, n)
                    nc.vector.tensor_tensor(split_parts[:, (n - 1) % 2, 2, :], split_rest[(n - 1) % 2],
                                            split_parts[:, (n - 1) % 2, 1, :], ALU.subtract).then_inc(part3_done, 1)
                if n == 0:
                    dve.wait_ge(consts_in, 16 * NCONST)
                    link(nc.vector.tensor_copy(w1_parts[:, 0, :], w1_rows[:, :]))
                    link(nc.vector.tensor_tensor(w1_rest[:, :], w1_rows[:, :], w1_parts[:, 0, :], ALU.subtract))
                    link(nc.vector.tensor_copy(w1_parts[:, 1, :], w1_rest[:, :]))
                    link(nc.vector.tensor_tensor(w1_parts[:, 2, :], w1_rest[:, :], w1_parts[:, 1, :], ALU.subtract))
                    for j in range(3):
                        hi = min(32 * (j + 1), W1R)
                        last = nc.vector.tensor_copy(w1_sb[32 * j:hi, :], w1_parts[32 * j:hi, j, :])
                    last.then_inc(w1_done, 1)
            dve.wait_ge(part3_done, NSPLIT)
            nc.vector.memset(agg, 0.0)
            nc.vector.memset(viol[:, :], 0.0)
            nc.vector.memset(eps[:, :], 1e-5)
            nc.vector.memset(ones[:, :], 1.0)
            dve.wait_ge(zeroed, 2)
            nc.vector.tensor_copy(col_f[:, :], col_i[:, :])
            link(nc.vector.tensor_copy(row_f[:, :], row_i[:, :]))
            link(nc.vector.tensor_scalar(ident[:, :], col_f[:, 0:P], row_f[:, 0:1], None, ALU.is_equal))
            dve.wait_ge(blocks_in, 16 * (1 + CPT))
            nc.vector.tensor_copy(mix[0:L, 0:L], ident[0:L, 0:L])
            link(nc.vector.memset(mix[2 * L:MX, L:MG], 1.0))
            dve.wait_ge(consts_in, 16 * NCONST)
            nc.vector.tensor_copy(base_f[:, :], base_all[:, :])
            link(nc.vector.tensor_copy(dst_f[:, :], dst_i))
            link(nc.vector.tensor_tensor(
                rel[:, :].rearrange("p (s t) -> p s t", t=TPS),
                dst_f[:, :].rearrange("p (s t) -> p s t", t=TPS),
                spread(base_f[:, :], 2, TPS), ALU.subtract))
            for n, (q, a, b) in enumerate(((P, 0, FULL), (REST, FULL, FULL + 1))):
                if q == 0 or a == b:
                    continue
                for lo in range(a, b, WIDE * TPS):
                    hi = min(lo + WIDE * TPS, b)
                    tmp = wide_onehot[:, :, :].rearrange("p t w -> p (t w)")[0:q, 0:hi - lo]
                    link(nc.vector.tensor_scalar(tmp, rel[0:q, lo:hi], 0.0, float(WIN - 1), ALU.max, ALU.min))
                    link(nc.vector.tensor_tensor(tmp, tmp, rel[0:q, lo:hi], ALU.not_equal))
                    link(nc.vector.tensor_reduce(viol[0:q, 1:2], tmp, AX.X, ALU.add))
                    link(nc.vector.tensor_tensor(viol[0:q, 0:1], viol[0:q, 0:1], viol[0:q, 1:2], ALU.add))
            nc.vector.tensor_copy(viol_all[:, :], viol[:, 0:1]).then_inc(setup_dve, 1)
            dve.wait_ge(flag_ps, 1)
            link(nc.vector.tensor_copy(flag[0:1, 0:1], ps_win[0:1, 0, 0:1]))
            n_setup = steps[0]
            dve.sem_inc(flag_set, 1)
            is_wide = dve.value_load(flag[0:1, 0:1], min_val=0, max_val=1 << 20)

            def onehots(it, h, passes):
                step_done(dve, win_done, HALF * (h + 1) - 1 - UNROLL, passes)
                nc.vector.tensor_tensor(
                    onehot[:, h, :, :], spread(col_f[:, 0:WIN], 1, HALF * TPS),
                    spread(rel[:, bass.ds((it * 2 + h) * HALF * TPS, HALF * TPS)], 2, WIN),
                    ALU.is_equal).then_inc(onehot_done[h], 1)

            def messages(s, passes, gathered):
                dve.wait_ge(x_in_sem[s], gathered)
                for h in range(2):
                    half_done(dve, w_done, s, h, passes)
                    if h == 0:
                        step_done(dve, msg_done, s - 2, passes)
                    nc.vector.tensor_tensor(
                        prod[:, 2 * (s % 2) + h, :, :, :],
                        ps_w[:, (2 * s + h) % 4, :].rearrange("p (t o i) -> p t o i", t=2, o=L),
                        spread(mx[:, s, 2 * h:2 * h + 2, L:2 * L], 2, L),
                        ALU.mult).then_inc(prod_done[2 * s + h], 1)
                for h in range(2):
                    half_done(dve, prod_done, s, h, passes)
                    last = nc.vector.tensor_reduce(mx[:, s, 2 * h:2 * h + 2, 0:L], prod[:, 2 * (s % 2) + h, :, :, :],
                                                   AX.X, ALU.add)
                last.then_inc(msg_done[s], 1)

            def add_window(s, base, passes):
                step_done(dve, win_done, s, passes)
                step_done(dve, agg_done, s - 1, passes)
                nc.vector.tensor_tensor(agg[:, bass.ds(base, WIN)], agg[:, bass.ds(base, WIN)],
                                        ps_win[0:MX, s % 2, 0:WIN], ALU.add).then_inc(agg_done[s], 1)

            def add_wide(d, it, u):
                itg = d * ITERS + it
                nc.vector.tensor_copy(shifted[:, :], dst_f[:, bass.ds((it * UNROLL + u) * TPS, TPS)]
                                      ).then_inc(shift_done[u % HALF], 1)
                with dve.Fori(0, NWIDE) as j:
                    n = (itg * 2 + u // HALF) * NWIDE + j
                    dve.wait_ge(shift_done[u % HALF], (itg * 2 + u // HALF) * (NWIDE + 1) + j + 1)
                    nc.vector.tensor_tensor(wide_onehot[:, :, :], spread(col_f[:, :], 1, TPS),
                                            spread(shifted[:, :], 2, WIDE),
                                            ALU.is_equal).then_inc(wide_onehot_done[u % HALF], 1)
                    dve.wait_ge(wide_win_done[u % HALF], n + 1)
                    nc.vector.tensor_tensor(agg[:, bass.ds(j * WIDE, WIDE)], agg[:, bass.ds(j * WIDE, WIDE)],
                                            ps_win[0:MX, u % 2, :], ALU.add).then_inc(wide_agg_done[u % HALF], 1)
                    dve.wait_ge(wide_onehot_done[u % HALF], n + 1)
                    dve.wait_ge(wide_agg_done[u % HALF], n + 1)
                    nc.vector.tensor_scalar(shifted[:, :], shifted[:, :], -float(WIDE), None,
                                            ALU.add).then_inc(shift_done[u % HALF], 1)
                dve.wait_ge(shift_done[u % HALF], (itg * 2 + u // HALF) * (NWIDE + 1) + (NWIDE + 1))
                dve.sem_inc(agg_done[u], 1)

            def depth_end(d):
                for j in range(NG):
                    acc = ps_w[:, j % 4, 0:CPG * MG].rearrange("p (c m) -> p c m", m=MG)
                    root = ps_w[:, j % 4, CPG * MG:CPG * (MG + L)].rearrange("p (c m) -> p c m", m=L)
                    dve.wait_ge(update_raw, d * NG + (j + 1))
                    k = d * (5 * NG) + (n_setup + 5 * j)
                    nc.vector.tensor_scalar(inv_deg[:, 0, :], acc[:, :, L:MG].rearrange("p c o -> p (c o)"),
                                            1.0, None, ALU.max).then_inc(dve_step, 1)
                    dve.wait_ge(dve_step, k + 1)
                    nc.vector.reciprocal(inv_deg[:, 1, :], inv_deg[:, 0, :]).then_inc(dve_step, 1)
                    dve.wait_ge(dve_step, k + 2)
                    nc.vector.tensor_tensor(mean_msg[:, :, :], acc[:, :, 0:L],
                                            spread(inv_deg[:, 1, :], 2, L),
                                            ALU.mult).then_inc(dve_step, 1)
                    dve.wait_ge(dve_step, k + 3)
                    nc.vector.tensor_tensor(mean_msg[:, :, :], mean_msg[:, :, :], root, ALU.add).then_inc(dve_step, 1)
                    dve.wait_ge(dve_step, k + 4)
                    dve.wait_ge(rows_done, d * NG + (NG + j - 1))
                    nc.vector.tensor_tensor(update[:, j % 2, :, :], mean_msg[:, :, :],
                                            root_b_sb[:, bass.ds(d, 1), :].broadcast_to([P, CPG, L]),
                                            ALU.add).then_inc(update_done, 1)
                    dve.wait_ge(update_done, d * NG + (j + 1))
                    dve.sem_inc(dve_step, 1)
                nc.vector.memset(agg, 0.0)

            with dve.Fori(0, DEPTH) as d:
                with dve.If(is_wide > 0):
                    with dve.Fori(0, ITERS) as it:
                        passes = pass_values(dve, d, it)
                        gathered = dve.snap((d * ITERS + it) * (16 * TPS) + 16 * TPS)
                        for u in range(UNROLL):
                            messages(u, passes, gathered)
                            add_wide(d, it, u)
                with dve.Else():
                    with dve.Fori(0, ITERS) as it:
                        passes = pass_values(dve, d, it)
                        gathered = dve.snap((d * ITERS + it) * (16 * TPS) + 16 * TPS)
                        _, bases = nc.values_load_multi_w_load_instructions(
                            base_sb[0:1, bass.ds(it * UNROLL, UNROLL)], engines=[mybir.EngineType.DVE],
                            min_val=0, max_val=NODES - WIN, skip_runtime_bounds_check_because="window starts are node numbers")
                        for u in range(UNROLL):
                            if u % HALF == 0:
                                onehots(it, u // HALF, passes)
                            messages(u, passes, gathered)
                            if u:
                                add_window(u - 1, bases[u - 1], passes)
                        add_window(UNROLL - 1, bases[UNROLL - 1], passes)
                depth_end(d)

            dve.wait_ge(rows_done, (DEPTH + 1) * NG)
            steps[0] = n_setup + 5 * NG * DEPTH
            link(nc.vector.tensor_tensor(rows[:, :, :], rows[:, :, :], x_in[:, :, :], ALU.add))
            link(nc.vector.tensor_reduce(stat[:, 0, :], rows[:, :, :], AX.X, ALU.add))
            link(nc.vector.tensor_scalar(stat[:, 0, :], stat[:, 0, :], 1.0 / L, None, ALU.mult))
            link(nc.vector.tensor_tensor(rows[:, :, :], rows[:, :, :],
                                         spread(stat[:, 0, :], 2, L), ALU.subtract))
            link(nc.vector.tensor_tensor(x_in[:, :, :], rows[:, :, :], rows[:, :, :], ALU.mult))
            nc.vector.tensor_reduce(stat[:, 1, :], x_in[:, :, :], AX.X, ALU.add).then_inc(var_done, 1)
            dve.wait_ge(std_done, 1)
            link(nc.vector.reciprocal(stat[:, 3, :], stat[:, 2, :]))
            nc.vector.tensor_tensor(x_in[:, :, :], rows[:, :, :],
                                    spread(stat[:, 3, :], 2, L), ALU.mult).then_inc(normed, 1)

        @block.tensor
        def _(pe):
            def layer1(s, passes, attr_passes):
                if s % HALF == 0:
                    pe.wait_ge(attr_landed[s // HALF % 2], attr_passes[s // UNROLL])
                step_done(pe, h1_done, s - 1, passes)
                nc.tensor.matmul(ps_h1[:, :], w1_sb[:, :], attr[:, s // HALF % 2, s % HALF * SE:(s % HALF + 1) * SE],
                                 start=True, stop=True).then_inc(h1_raw[s % UNROLL], 1)

            def layer2(s, passes):
                step_done(pe, h1_done, s, passes)
                step_done(pe, h2_done, s - 1, passes)
                nc.tensor.matmul(ps_h2[:, :], w2_sb[:, :], h1[:, s % 2, :],
                                 start=True, stop=True).then_inc(h2_raw[s % UNROLL], 1)

            def layer3(s, h, passes):
                if h == 0:
                    step_done(pe, h2_done, s, passes)
                half_done(pe, prod_done, s - 2, h, passes)
                for t in range(2):
                    last = nc.tensor.matmul(ps_w[:, (2 * s + h) % 4, t * L * L:(t + 1) * L * L],
                                            h2[:, s % 2, (2 * h + t) * P:(2 * h + t + 1) * P], w3_sb[:, :],
                                            start=True, stop=True)
                last.then_inc(w_done[2 * s + h], 1)

            def scatter(s, passes):
                step_done(pe, msg_done, s, passes)
                if s % HALF == 0:
                    pe.wait_ge(onehot_done[s // HALF], passes[0])
                step_done(pe, agg_done, s - 2, passes)
                for t in range(TPS):
                    last = nc.tensor.matmul(ps_win[0:MX, s % 2, 0:WIN], mx[:, s, t, :],
                                            onehot[:, s // HALF, s % HALF * TPS + t, :],
                                            start=(t == 0), stop=(t == TPS - 1))
                last.then_inc(win_done[s], 1)

            def scatter_wide(s, n, passes):
                step_done(pe, msg_done, s, passes)
                pe.sem_inc(pe_turns, 1)
                with pe.Fori(0, NWIDE) as j:
                    pe.wait_ge(wide_onehot_done[s % HALF], n * NWIDE + j + 1)
                    for t in range(TPS):
                        last = nc.tensor.matmul(ps_win[0:MX, s % 2, :], mx[:, s, t, :],
                                                wide_onehot[:, t, :], start=(t == 0), stop=(t == TPS - 1))
                    last.then_inc(wide_win_done[s % HALF], 1)
                pe.wait_ge(wide_agg_done[s % HALF], n * NWIDE + NWIDE)
                pe.sem_inc(win_done[s], 1)

            pe.wait_ge(w1_done, 1)
            pe.wait_ge(setup_dve, 1)
            nc.tensor.matmul(ps_win[0:1, 0, 0:1], viol_all[:, :], ones[:, :], start=True, stop=True).then_inc(flag_ps, 1)
            for sems in (h1_raw, h1_done, h2_raw, h2_done, w_done, prod_done, msg_done, onehot_done, win_done, agg_done):
                for s in sems:
                    pe.sem_inc(s, LEAD)
            pe.wait_ge(flag_set, 1)
            is_wide = pe.value_load(flag[0:1, 0:1], min_val=0, max_val=1 << 20)
            first = {-1: LEAD, 0: LEAD + 1}
            layer1(0, first, {0: 48})
            layer1(1, first, None)
            layer2(0, first)
            with pe.Fori(0, DEPTH) as d:
                pe.wait_ge(rows_done, d * NG + NG)
                for k in range(NTB):
                    if k >= 2:
                        pe.wait_ge(rows_t_done, d * NTB + (k - 1))
                    for a in range(TB * k, min(TB * (k + 1), NT)):
                        last = nc.tensor.transpose(
                            ps_win[0:CPT * L, k % 2, (a % TB) * P:(a % TB + 1) * P],
                            rows[:, CPT * a:CPT * (a + 1), :].rearrange("p c i -> p (c i)"), ident[:, :])
                    last.then_inc(transposed, 1)
                pe.wait_ge(rows_t_done, d * NTB + NTB)
                pe.sem_inc(pe_turns, 1)
                with pe.If(is_wide > 0):
                    with pe.Fori(0, ITERS) as it:
                        passes = pass_values(pe, d, it)
                        attr_passes = {k: (d * ITERS + it) * 48 + 48 * (k + 1) for k in (0, 1)}
                        for u in range(UNROLL):
                            layer3(u, 0, passes)
                            layer2(u + 1, passes)
                            layer3(u, 1, passes)
                            layer1(u + 2, passes, attr_passes)
                            scatter_wide(u, (d * ITERS + it) * 2 + u // HALF, passes)
                with pe.Else():
                    with pe.Fori(0, ITERS) as it:
                        passes = pass_values(pe, d, it)
                        attr_passes = {k: (d * ITERS + it) * 48 + 48 * (k + 1) for k in (0, 1)}
                        for u in range(UNROLL):
                            layer3(u, 0, passes)
                            layer2(u + 1, passes)
                            if u:
                                scatter(u - 1, passes)
                            layer3(u, 1, passes)
                            layer1(u + 2, passes, attr_passes)
                        scatter(UNROLL - 1, passes)
                pe.wait_ge(agg_done[UNROLL - 1], d * ITERS + (LEAD + ITERS))
                for j in range(NG):
                    if j >= 4:
                        pe.wait_ge(update_done, d * NG + (j - 3))
                    for c in range(CPG):
                        nc.tensor.matmul(ps_w[:, j % 4, c * MG:(c + 1) * MG],
                                         agg[:, bass.ds(CPG * j + c, P, step=NB)], mix[:, :],
                                         start=True, stop=True)
                    for r in range(CPG // CPT):
                        at = CPG * MG + r * CPT * L
                        last = nc.tensor.matmul(ps_w[:, j % 4, at:at + CPT * L],
                                                rows_t[:, (CPG // CPT) * j + r, :],
                                                root_blocks[:, bass.ds(d, 1), :].rearrange("p d n -> p (d n)"),
                                                start=True, stop=True)
                    last.then_inc(update_raw, 1)


def kernel(x, src, dst, edge_attr_6, L0_gnn_kW1, L0_gnn_kb1, L0_gnn_kW2, L0_gnn_kb2, L0_gnn_kW3, L0_gnn_kb3,
           L0_gnn_root_W, L0_gnn_root_b):
    import numpy as np
    import concourse.bacc as bacc
    from concourse import mybir
    from concourse.bass_utils import run_bass_kernel_spmd

    x, src, dst, edge_attr = (np.asarray(a) for a in (x, src, dst, edge_attr_6))
    n, l = x.shape
    e = src.shape[0]
    nb, iters = sizes(n, e)
    slots = iters * UNROLL * SE
    extra = 2 * HALF * SE

    x_rows = np.zeros((P * nb, l), x.dtype)
    x_rows[:n] = x
    attr = np.zeros((slots + extra, edge_attr.shape[1]), edge_attr.dtype)
    attr[:e] = edge_attr
    attr[slots:] = attr[:extra]
    attr_in = attr.reshape(iters + 1, UNROLL * SE, -1).transpose(0, 2, 1)
    src_pad = np.zeros(slots + extra, src.dtype)
    src_pad[:e] = src
    src_pad[slots:] = src_pad[:extra]
    src_idx = src_pad.reshape(-1, HALF * TPS, P).transpose(0, 2, 1)
    dst_pad = np.full(slots, -1, dst.dtype)
    dst_pad[:e] = dst
    dst_tiles = dst_pad.reshape(-1, P).T
    base_row = np.zeros((1, slots // SE), dst.dtype)
    first = dst_pad[::SE]
    used = -(-e // SE)
    base_row[0, :used] = first[:used]
    w3 = np.asarray(L0_gnn_kW3).reshape(-1, l, l).transpose(0, 2, 1).reshape(-1, l * l)
    arrays = dict(
        x_rows=x_rows.reshape(P, nb * l), attr_in=attr_in, src_idx=src_idx, dst_tiles=dst_tiles, base_row=base_row,
        w1=L0_gnn_kW1, b1=np.asarray(L0_gnn_kb1).reshape(-1, 1), w2=L0_gnn_kW2,
        b2=np.asarray(L0_gnn_kb2).reshape(-1, 1), w3=w3, b3=np.asarray(L0_gnn_kb3).reshape(l, l),
        root_w=L0_gnn_root_W, root_b=L0_gnn_root_b)
    arrays = {k: np.ascontiguousarray(v) for k, v in arrays.items()}

    nc = bacc.Bacc("TRN2", target_bir_lowering=False, num_devices=1)
    ins = {k: nc.dram_tensor(k, v.shape, mybir.dt.from_np(v.dtype), kind="ExternalInput").ap()
           for k, v in arrays.items()}
    out = nc.dram_tensor("out", (P, nb * l), mybir.dt.float32, kind="ExternalOutput").ap()
    gnn_resnorm_kernel(nc, **ins, out=out, n_edges=e)
    r = run_bass_kernel_spmd(nc, [arrays], core_ids=[0])
    return r.results[0]["out"].reshape(P * nb, l)[:n]
```

```python
import concourse.bass as bass
from concourse import mybir
from contextlib import ExitStack

P = 128
TPS = 4
SE = TPS * P
UNROLL = 8
HALF = UNROLL // 2
WIN = 32
WIDE = 512
CPG = 28
CPT = 7
LEAD = 1


def sizes(n_nodes, n_edges):
    chunks = -(-n_nodes // (P * CPT)) * CPT
    iters = -(-n_edges // (SE * UNROLL))
    return chunks, iters


def spread(ap, axis, n):
    shape = list(ap.shape)
    return ap.unsqueeze(axis).broadcast_to(shape[:axis] + [n] + shape[axis:])


def gnn_resnorm_kernel(nc, x_rows, attr_in, src_idx, dst_tiles, base_row, w1, b1, w2, b2, w3, b3,
                       root_w, root_b, out, n_edges):
    fp32, i32, bf16 = mybir.dt.float32, mybir.dt.int32, mybir.dt.bfloat16
    ALU = mybir.AluOpType
    ACT = mybir.ActivationFunctionType
    AX = mybir.AxisListType

    L = 16
    EDIM, K = w1.shape
    DEPTH = root_w.shape[0]
    NB = x_rows.shape[1] // L
    NODES = P * NB
    groups = [(c, min(CPG, NB - c)) for c in range(0, NB, CPG)]
    NG = len(groups)
    NT = NB // CPT
    TB = 4
    t_banks = [(a, min(TB, NT - a)) for a in range(0, NT, TB)]
    NTB = len(t_banks)
    assert NTB <= 4
    NWIDE = -(-NODES // WIDE)
    TILES = dst_tiles.shape[1]
    SUPERS = TILES // TPS
    ITERS = SUPERS // UNROLL
    MX = 2 * L + 1
    MG = L + 1
    FULL, REST = n_edges // P, n_edges % P

    table = nc.dram_tensor("node_table", (NODES, L), fp32, kind="Internal").ap()
    PASSES = attr_in.shape[0]
    PASS_E = UNROLL * SE
    SEG = 16
    SEGW = PASS_E // SEG
    AHEAD = 2
    W1R = 2 * 32 + 3 * EDIM
    B3R = 2 * 32 + 1
    attr_parts = nc.dram_tensor("attr_parts", (PASSES, 3 * EDIM, PASS_E), bf16, kind="Internal").ap()
    table_rows = table.rearrange("(p c) i -> p (c i)", p=P)

    ctx = ExitStack()
    with ctx:
        def sb(name, shape, dt=fp32):
            return ctx.enter_context(nc.sbuf_tensor(name, shape, dt))

        def pb(name, shape):
            return ctx.enter_context(nc.psum_tensor(name, shape, fp32))

        def sem(name):
            return ctx.enter_context(nc.semaphore(name))

        w1_rows = sb("w1_rows", [W1R, K])
        w1_rest = sb("w1_rest", [W1R, K])
        w1_parts = sb("w1_parts", [W1R, 3, K], bf16)
        w1_sb = sb("w1_sb", [W1R, K], bf16)
        w2_sb = sb("w2_sb", [K, K])
        w3_sb = sb("w3_sb", [K, L * L])
        b1_sb = sb("b1_sb", [K, 1])
        b2_sb = sb("b2_sb", [K, 1])
        root_b_sb = sb("root_b_sb", [P, DEPTH, L])
        b3_in = sb("b3_in", [B3R, L * L])
        b3_rest = sb("b3_rest", [B3R, L * L])
        b3_cut = sb("b3_cut", [B3R, 3, L * L], bf16)
        b3_parts = sb("b3_parts", [B3R, 2, L * L], bf16)
        b3_ones = sb("b3_ones", [B3R, P], bf16)
        root_blocks = sb("root_blocks", [CPT * L, DEPTH, CPT * L])
        attr = sb("attr", [W1R, 2, HALF * SE], bf16)
        split_in = sb("split_in", [EDIM * SEG, AHEAD, SEGW])
        split_rest = sb("split_rest", [EDIM * SEG, AHEAD, SEGW])
        split_parts = sb("split_parts", [EDIM * SEG, 3, AHEAD, SEGW], bf16)
        idx = sb("idx", [P, 2, HALF * TPS], i32)
        h1 = sb("h1", [K, 2, SE])
        h2 = sb("h2", [K, 2, SE])
        prod = sb("prod", [P, 4, 2, L, L])
        mx = sb("mx", [P, UNROLL, TPS, MX])
        onehot = sb("onehot", [P, 2, HALF * TPS, WIN])
        shifted = sb("shifted", [P, TPS])
        wide_onehot = sb("wide_onehot", [P, TPS, WIDE])
        rel = sb("rel", [P, TILES])
        dst_i = sb("dst_i", [P, TILES], i32)
        base_all = sb("base_all", [P, SUPERS], i32)
        base_sb = sb("base_sb", [1, SUPERS], i32)
        agg = sb("agg", [MG, NWIDE * WIDE])
        rows = sb("rows", [P, NB, L])
        x_in = sb("x_in", [P, NB, L])
        squares = sb("squares", [P, NB, L])
        rows_t = sb("rows_t", [CPT * L, NTB * TB, P])
        update = sb("update", [P, 2, CPG, L])
        mean_msg = sb("mean_msg", [P, 2, CPG, L])
        root_sum = sb("root_sum", [P, NB, L])
        inv_deg = sb("inv_deg", [P, 2, CPG])
        ident = sb("ident", [P, P])
        col_i = sb("col_i", [P, WIDE], i32)
        col_f = sb("col_f", [P, WIDE])
        row_i = sb("row_i", [P, 1], i32)
        row_f = sb("row_f", [P, 1])
        ones = sb("ones", [P, 1])
        eps = sb("eps", [P, 1])
        outside = sb("outside", [P, 2])
        any_outside = sb("any_outside", [P, 1])
        flag = sb("flag", [1, 1], i32)
        stat = sb("stat", [P, 4, NB])

        ps_h1 = pb("ps_h1", [P, SE])
        ps_h2 = pb("ps_h2", [P, SE])
        ps_w = pb("ps_w", [P, 4, 512])
        ps_win = pb("ps_win", [P, 2, 512])

        pool_turns = sem("pool_turns")
        pe_turns = sem("pe_turns")
        dst_in = sem("dst_in")
        consts_in = sem("consts_in")
        zeroed = sem("zeroed")
        blocks_in = sem("blocks_in")
        dve_step = sem("dve_step")
        setup_dve = sem("setup_dve")
        flag_ps = sem("flag_ps")
        flag_set = sem("flag_set")
        attr_landed = [sem(f"attr_landed{h}") for h in range(2)]
        split_loaded = sem("split_loaded")
        parts_written = sem("parts_written")
        rows_loaded = sem("rows_loaded")
        x_loaded = sem("x_loaded")
        sp_turns = sem("sp_turns")
        part1_done = sem("part1_done")
        rest_done = sem("rest_done")
        part2_done = sem("part2_done")
        part3_done = sem("part3_done")
        w1_done = sem("w1_done")
        idx_in = [sem(f"idx_in{h}") for h in range(2)]
        x_gathered = [sem(f"x_gathered{u}") for u in range(UNROLL)]
        h1_raw = [sem(f"h1_raw{u}") for u in range(UNROLL)]
        h1_done = [sem(f"h1_done{u}") for u in range(UNROLL)]
        h2_raw = [sem(f"h2_raw{u}") for u in range(UNROLL)]
        h2_done = [sem(f"h2_done{u}") for u in range(UNROLL)]
        w_done = [sem(f"w_done{q}") for q in range(2 * UNROLL)]
        prod_done = [sem(f"prod_done{q}") for q in range(2 * UNROLL)]
        msg_done = [sem(f"msg_done{u}") for u in range(UNROLL)]
        onehot_done = [sem(f"onehot_done{h}") for h in range(2)]
        win_done = [sem(f"win_done{u}") for u in range(UNROLL)]
        agg_done = [sem(f"agg_done{u}") for u in range(UNROLL)]
        wide_onehot_done = [sem(f"wide_onehot_done{u}") for u in range(HALF)]
        wide_win_done = [sem(f"wide_win_done{u}") for u in range(HALF)]
        wide_agg_done = [sem(f"wide_agg_done{u}") for u in range(HALF)]
        shift_done = [sem(f"shift_done{u}") for u in range(HALF)]
        transposed = sem("transposed")
        rows_t_done = sem("rows_t_done")
        root_raw = sem("root_raw")
        root_done = sem("root_done")
        update_raw = sem("update_raw")
        update_done = sem("update_done")
        rows_done = sem("rows_done")
        table_written = sem("table_written")
        var_done = sem("var_done")
        std_done = sem("std_done")
        normed = sem("normed")
        out_written = sem("out_written")

        NCONST = 6 + 9

        def pass_values(eng, d, it):
            n = d * ITERS + it
            return {k: eng.snap(n + (LEAD + 1 + k)) for k in (-1, 0, 1)}

        def step_done(eng, sems, s, passes):
            eng.wait_ge(sems[s % UNROLL], passes[s // UNROLL])

        def half_done(eng, sems, s, h, passes):
            eng.wait_ge(sems[2 * (s % UNROLL) + h], passes[s // UNROLL])

        block = ctx.enter_context(nc.Block())

        @block.sync
        def _(sp):
            sp.dma_start(table_rows, x_rows).then_inc(table_written, 16)
            for h in range(2):
                sp.dma_start(idx[:, h, :], src_idx[h, :, :]).then_inc(idx_in[h], 16)
            sp.dma_start(split_in[:, :, :], attr_in[0:AHEAD, :, :].rearrange("q e (s w) -> (e s) q w", w=SEGW)
                         ).then_inc(split_loaded, 16)

            def attr_load(h, at):
                for j in range(3):
                    sp.dma_start(attr[32 * j:32 * j + 3 * EDIM, h, :],
                                 attr_parts[at, :, h * HALF * SE:(h + 1) * HALF * SE]
                                 ).then_inc(attr_landed[h], 16)

            for dst, src in ((dst_i[:, :], dst_tiles), (base_sb[:, :], base_row),
                             (base_all[:, :], base_row.broadcast_to([P, SUPERS]))):
                sp.dma_start(dst, src).then_inc(dst_in, 16)
            for dst, src in ((w2_sb[:, :], w2), (w3_sb[:, :], w3), (b3_in[:, :], b3.broadcast_to([B3R, L * L])),
                             (b1_sb[:, :], b1), (b2_sb[:, :], b2),
                             (root_b_sb[:, :, :], root_b.rearrange("(o d) i -> o d i", o=1).broadcast_to([P, DEPTH, L]))):
                sp.dma_start(dst, src).then_inc(consts_in, 16)
            sp.wait_ge(zeroed, 1)
            for b in range(3):
                for i in range(3):
                    at = 32 * b + i * EDIM
                    sp.dma_start(w1_rows[at:at + EDIM, :], w1).then_inc(consts_in, 16)
            sp.dma_start(rows[:, :, :].rearrange("p c i -> p (c i)"), x_rows).then_inc(rows_loaded, 16)
            sp.wait_ge(part3_done, 1)
            for i in range(3):
                sp.dma_start(attr_parts[0:AHEAD, i * EDIM:(i + 1) * EDIM, :]
                             .rearrange("q e (s w) -> (e s) q w", w=SEGW),
                             split_parts[:, i, :, :]).then_inc(parts_written, 16)
            sp.wait_ge(parts_written, 48)
            attr_load(0, 0)
            attr_load(1, 0)
            sp.dma_start(x_in[:, :, :].rearrange("p c i -> p (c i)"), x_rows).then_inc(x_loaded, 16)
            for b in range(CPT):
                sp.dma_start(root_blocks[b * L:(b + 1) * L, :, b * L:(b + 1) * L],
                             root_w.rearrange("d i o -> i d o")).then_inc(blocks_in, 16)
            with sp.Fori(0, DEPTH) as d:
                with sp.Fori(0, ITERS) as it:
                    passes = pass_values(sp, d, it)
                    parts_before = sp.snap((d * ITERS + it) * 48 + 48)
                    sp.wait_ge(rest_done, passes[-1])
                    sp.wait_ge(parts_written, parts_before)
                    sp.sem_inc(sp_turns, 1)
                    sp.dma_start(split_in[:, 0:1, :], attr_in[bass.ds(it + AHEAD, 1), :, :]
                                 .rearrange("q e (s w) -> (e s) q w", w=SEGW)).then_inc(split_loaded, 16)
                    for h in range(2):
                        step_done(sp, h1_raw, HALF * (h + 1) - 1, passes)
                        for j in range(3):
                            sp.dma_start(attr[32 * j:32 * j + 3 * EDIM, h, :],
                                         attr_parts[bass.ds(it + 1, 1), :, h * HALF * SE:(h + 1) * HALF * SE]
                                         .rearrange("q r n -> (q r) n")).then_inc(attr_landed[h], 16)
                        for u in range(HALF * h, HALF * (h + 1)):
                            sp.wait_ge(x_gathered[u], (d * ITERS + it) * (16 * TPS) + 16 * TPS)
                        sp.dma_start(idx[:, h, :], src_idx[bass.ds(it * 2 + (2 + h), 1), :, :]
                                     .rearrange("c p n -> (c p) n")).then_inc(idx_in[h], 16)
                    sp.wait_ge(part3_done, passes[0])
                    sp.sem_inc(sp_turns, 1)
                    for i in range(3):
                        sp.dma_start(attr_parts[bass.ds(it + AHEAD, 1), i * EDIM:(i + 1) * EDIM, :]
                                     .rearrange("q e (s w) -> (e s) q w", w=SEGW),
                                     split_parts[:, i, 0:1, :]).then_inc(parts_written, 16)
                sp.wait_ge(rows_done, d * NG + 2 * NG)
                sp.dma_start(table_rows, rows[:, :, :].rearrange("p c i -> p (c i)")).then_inc(table_written, 16)
            for h in range(2):
                sp.wait_ge(attr_landed[h], 48 * (DEPTH * ITERS + 1))
                sp.wait_ge(idx_in[h], 16 * (DEPTH * ITERS + 1))
            sp.wait_ge(normed, 1)
            sp.dma_start(out, x_in[:, :, :].rearrange("p c i -> p (c i)")).then_inc(out_written, 16)
            sp.wait_ge(table_written, 16 * (DEPTH + 1))
            sp.wait_ge(parts_written, 48 * (DEPTH * ITERS + 1))
            sp.wait_ge(out_written, 16)

        @block.gpsimd
        def _(pool):
            nc.gpsimd.memset(b3_parts[:, :, :], 0.0)
            nc.gpsimd.memset(b3_ones[:, :], 1.0)
            nc.gpsimd.memset(root_blocks[:, :, :], 0.0)
            nc.gpsimd.iota(col_i[:, :], pattern=[[1, WIDE]], base=0, channel_multiplier=0)
            nc.gpsimd.iota(row_i[:, :], pattern=[[1, 1]], base=0, channel_multiplier=1)
            nc.gpsimd.memset(attr[:, :, :], 0.0)
            nc.gpsimd.memset(w1_rows[:, :], 0.0)
            nc.gpsimd.memset(mx[:, :, :, :], 1.0).then_inc(zeroed, 1)
            pool.wait_ge(zeroed, 1)
            with pool.Fori(0, DEPTH) as d:
                pool.wait_ge(table_written, d * 16 + 16)
                pool.sem_inc(pool_turns, 1)
                with pool.Fori(0, ITERS) as it:
                    passes = pass_values(pool, d, it)
                    for u in range(UNROLL):
                        if u % HALF == 0:
                            pool.wait_ge(idx_in[u // HALF], (d * ITERS + it) * 16 + 16)
                        step_done(pool, win_done, u - UNROLL, passes)
                        pool.sem_inc(pool_turns, 1)
                        for t in range(TPS):
                            c = (u % HALF) * TPS + t
                            nc.gpsimd.indirect_dma_start(
                                out=mx[:, u, t, 0:L], out_offset=None, in_=table,
                                in_offset=bass.IndirectOffsetOnAxis(ap=idx[:, u // HALF, c:c + 1], axis=0),
                            ).then_inc(x_gathered[u], 16)

        @block.scalar
        def _(act):
            def split_part(i, src, n, ready, value, done):
                act.wait_ge(ready, value)
                nc.scalar.copy(split_parts[:, i, 0:n, :], src[:, 0:n, :]).then_inc(done, 1)

            split_part(0, split_in, AHEAD, split_loaded, 16, part1_done)
            split_part(1, split_rest, AHEAD, rest_done, 1, part2_done)
            act.wait_ge(consts_in, 16 * NCONST)

            first = {-1: LEAD, 0: LEAD + 1}

            def gelu1(s, passes):
                step_done(act, h1_raw, s, passes)
                step_done(act, h2_raw, s - 2, passes)
                nc.scalar.activation(h1[:, s % 2, :], ps_h1[:, :], ACT.Gelu_apprx_tanh,
                                     bias=b1_sb[:, 0:1]).then_inc(h1_done[s % UNROLL], 1)

            def gelu2(s, passes):
                step_done(act, h2_raw, s, passes)
                half_done(act, w_done, s - 2, 1, passes)
                nc.scalar.activation(h2[:, s % 2, :], ps_h2[:, :], ACT.Gelu_apprx_tanh,
                                     bias=b2_sb[:, 0:1]).then_inc(h2_done[s % UNROLL], 1)

            gelu1(0, first)
            gelu1(1, first)
            gelu2(0, first)
            with act.Fori(0, DEPTH) as d:
                for k, (a, n) in enumerate(t_banks):
                    act.wait_ge(transposed, d * NTB + (k + 1))
                    nc.scalar.copy(rows_t[:, a:a + n, :],
                                   ps_win[0:CPT * L, k % 2, 0:n * P].rearrange("p (a b) -> p a b", b=P)
                                   ).then_inc(rows_t_done, 1)
                with act.Fori(0, ITERS) as it:
                    passes = pass_values(act, d, it)
                    for u in range(UNROLL):
                        gelu2(u + 1, passes)
                        gelu1(u + 2, passes)
                        if u == 2:
                            split_part(0, split_in, 1, split_loaded, (d * ITERS + it) * 16 + 32, part1_done)
                        if u == 4:
                            split_part(1, split_rest, 1, rest_done, passes[0], part2_done)
                for j, (c, n) in enumerate(groups):
                    act.wait_ge(update_done, d * NG + (j + 1))
                    nc.scalar.activation(rows[:, c:c + n, :], update[:, j % 2, 0:n, :],
                                         ACT.Gelu_apprx_tanh).then_inc(rows_done, 1)
            act.wait_ge(var_done, 1)
            nc.scalar.activation(stat[:, 2, :], stat[:, 1, :], ACT.Sqrt, bias=eps[:, 0:1],
                                 scale=1.0 / L).then_inc(std_done, 1)

        @block.vector
        def _(dve):
            steps = [0]

            def link(ins):
                steps[0] += 1
                ins.then_inc(dve_step, 1)
                dve.wait_ge(dve_step, steps[0])

            def split_rest_of_first(n, value):
                dve.wait_ge(part1_done, value)
                nc.vector.tensor_tensor(split_rest[:, 0:n, :], split_in[:, 0:n, :], split_parts[:, 0, 0:n, :],
                                        ALU.subtract).then_inc(rest_done, 1)

            def split_third(n, value):
                dve.wait_ge(part2_done, value)
                nc.vector.tensor_tensor(split_parts[:, 2, 0:n, :], split_rest[:, 0:n, :], split_parts[:, 1, 0:n, :],
                                        ALU.subtract).then_inc(part3_done, 1)

            nc.vector.memset(agg[:, 0:NWIDE * WIDE // 2], 0.0)
            split_rest_of_first(AHEAD, 1)
            split_third(AHEAD, 1)
            nc.vector.memset(outside[:, :], 0.0)
            nc.vector.memset(eps[:, :], 1e-5)
            nc.vector.memset(ones[:, :], 1.0)
            dve.wait_ge(zeroed, 1)
            dve.wait_ge(dst_in, 16 * 3)
            link(nc.vector.tensor_tensor(
                rel[:, :].rearrange("p (s t) -> p s t", t=TPS),
                dst_i[:, :].rearrange("p (s t) -> p s t", t=TPS),
                spread(base_all[:, :], 2, TPS), ALU.subtract))
            for q, a, b in ((P, 0, FULL), (REST, FULL, FULL + 1)):
                if q == 0 or a == b:
                    continue
                for lo in range(a, b, WIDE * TPS):
                    hi = min(lo + WIDE * TPS, b)
                    tmp = wide_onehot[:, :, :].rearrange("p t w -> p (t w)")[0:q, 0:hi - lo]
                    link(nc.vector.scalar_tensor_tensor(tmp, rel[0:q, lo:hi], -float(WIN - 1), rel[0:q, lo:hi],
                                                        ALU.add, ALU.mult))
                    link(nc.vector.tensor_reduce(outside[0:q, 1:2], tmp, AX.X, ALU.max))
                    link(nc.vector.tensor_tensor(outside[0:q, 0:1], outside[0:q, 0:1], outside[0:q, 1:2], ALU.max))
            nc.vector.tensor_scalar(any_outside[:, :], outside[:, 0:1], 0.0, None, ALU.is_gt).then_inc(setup_dve, 1)
            nc.vector.tensor_copy(col_f[:, :], col_i[:, :])
            link(nc.vector.tensor_copy(row_f[:, :], row_i[:, :]))
            link(nc.vector.tensor_scalar(ident[:, :], col_f[:, 0:P], row_f[:, 0:1], None, ALU.is_equal))
            dve.wait_ge(consts_in, 16 * NCONST)
            link(nc.vector.tensor_copy(w1_parts[:, 0, :], w1_rows[:, :]))
            link(nc.vector.tensor_tensor(w1_rest[:, :], w1_rows[:, :], w1_parts[:, 0, :], ALU.subtract))
            link(nc.vector.tensor_copy(w1_parts[:, 1, :], w1_rest[:, :]))
            link(nc.vector.tensor_tensor(w1_parts[:, 2, :], w1_rest[:, :], w1_parts[:, 1, :], ALU.subtract))
            link(nc.vector.tensor_copy(b3_cut[:, 0, :], b3_in[:, :]))
            link(nc.vector.tensor_tensor(b3_rest[:, :], b3_in[:, :], b3_cut[:, 0, :], ALU.subtract))
            link(nc.vector.tensor_copy(b3_cut[:, 1, :], b3_rest[:, :]))
            link(nc.vector.tensor_tensor(b3_cut[:, 2, :], b3_rest[:, :], b3_cut[:, 1, :], ALU.subtract))
            for j in range(3):
                nc.vector.tensor_copy(b3_parts[32 * j:32 * j + 1, :, :],
                                      spread(b3_cut[32 * j:32 * j + 1, j, :], 1, 2))
            for j in range(3):
                hi = min(32 * (j + 1), W1R)
                last = nc.vector.tensor_copy(w1_sb[32 * j:hi, :], w1_parts[32 * j:hi, j, :])
            last.then_inc(w1_done, 1)
            dve.wait_ge(flag_ps, 1)
            link(nc.vector.tensor_copy(flag[0:1, 0:1], ps_win[0:1, 0, 0:1]))
            dve.sem_inc(flag_set, 1)
            nc.vector.memset(agg[:, NWIDE * WIDE // 2:], 0.0)
            n_setup = steps[0]
            is_wide = dve.value_load(flag[0:1, 0:1], min_val=0, max_val=1 << 20)

            def split_step(u, passes):
                if u == 3:
                    split_rest_of_first(1, passes[0])
                if u == 5:
                    split_third(1, passes[0])

            def onehots(it, h, passes):
                step_done(dve, win_done, HALF * (h + 1) - 1 - UNROLL, passes)
                nc.vector.tensor_tensor(
                    onehot[:, h, :, :], spread(col_f[:, 0:WIN], 1, HALF * TPS),
                    spread(rel[:, bass.ds((it * 2 + h) * HALF * TPS, HALF * TPS)], 2, WIN),
                    ALU.is_equal).then_inc(onehot_done[h], 1)

            def messages(s, passes, gathered):
                dve.wait_ge(x_gathered[s], gathered)
                for h in range(2):
                    half_done(dve, w_done, s, h, passes)
                    if h == 0:
                        step_done(dve, msg_done, s - 2, passes)
                    nc.vector.tensor_tensor(
                        prod[:, 2 * (s % 2) + h, :, :, :],
                        ps_w[:, (2 * s + h) % 4, :].rearrange("p (t o i) -> p t o i", t=2, o=L),
                        spread(mx[:, s, 2 * h:2 * h + 2, 0:L], 2, L),
                        ALU.mult).then_inc(prod_done[2 * s + h], 1)
                for h in range(2):
                    half_done(dve, prod_done, s, h, passes)
                    last = nc.vector.tensor_reduce(mx[:, s, 2 * h:2 * h + 2, L:2 * L], prod[:, 2 * (s % 2) + h, :, :, :],
                                                   AX.X, ALU.add)
                last.then_inc(msg_done[s], 1)

            def add_window(s, base, passes):
                step_done(dve, win_done, s, passes)
                step_done(dve, agg_done, s - 1, passes)
                nc.vector.tensor_tensor(agg[:, bass.ds(base, WIN)], agg[:, bass.ds(base, WIN)],
                                        ps_win[0:MG, s % 2, 0:WIN], ALU.add).then_inc(agg_done[s], 1)

            def add_wide(d, it, u):
                itg = d * ITERS + it
                nc.vector.tensor_copy(shifted[:, :], dst_i[:, bass.ds((it * UNROLL + u) * TPS, TPS)]
                                      ).then_inc(shift_done[u % HALF], 1)
                with dve.Fori(0, NWIDE) as j:
                    n = (itg * 2 + u // HALF) * NWIDE + j
                    dve.wait_ge(shift_done[u % HALF], (itg * 2 + u // HALF) * (NWIDE + 1) + j + 1)
                    nc.vector.tensor_tensor(wide_onehot[:, :, :], spread(col_f[:, :], 1, TPS),
                                            spread(shifted[:, :], 2, WIDE),
                                            ALU.is_equal).then_inc(wide_onehot_done[u % HALF], 1)
                    dve.wait_ge(wide_win_done[u % HALF], n + 1)
                    nc.vector.tensor_tensor(agg[:, bass.ds(j * WIDE, WIDE)], agg[:, bass.ds(j * WIDE, WIDE)],
                                            ps_win[0:MG, u % 2, :], ALU.add).then_inc(wide_agg_done[u % HALF], 1)
                    dve.wait_ge(wide_onehot_done[u % HALF], n + 1)
                    dve.wait_ge(wide_agg_done[u % HALF], n + 1)
                    nc.vector.tensor_scalar(shifted[:, :], shifted[:, :], -float(WIDE), None,
                                            ALU.add).then_inc(shift_done[u % HALF], 1)
                dve.wait_ge(shift_done[u % HALF], (itg * 2 + u // HALF) * (NWIDE + 1) + (NWIDE + 1))
                dve.sem_inc(agg_done[u], 1)

            def root_sums(d):
                for k, (a, n) in enumerate(t_banks):
                    dve.wait_ge(root_raw, d * NTB + (k + 1))
                    nc.vector.tensor_tensor(root_sum[:, a * CPT:(a + n) * CPT, :],
                                            ps_w[:, k, 0:n * CPT * L].rearrange("p (c i) -> p c i", i=L),
                                            root_b_sb[:, bass.ds(d, 1), :].broadcast_to([P, n * CPT, L]),
                                            ALU.add).then_inc(root_done, 1)

            def depth_end(d):
                for j, (c, n) in enumerate(groups):
                    acc = ps_w[:, j % 4, 0:n * MG].rearrange("p (c m) -> p c m", m=MG)
                    dve.wait_ge(update_raw, d * NG + (j + 1))
                    k = d * (4 * NG) + (n_setup + 4 * j)
                    nc.vector.tensor_scalar(inv_deg[:, 0, 0:n], acc[:, :, L:MG].rearrange("p c o -> p (c o)"),
                                            1.0, None, ALU.max).then_inc(dve_step, 1)
                    dve.wait_ge(dve_step, k + 1)
                    nc.vector.reciprocal(inv_deg[:, 1, 0:n], inv_deg[:, 0, 0:n]).then_inc(dve_step, 1)
                    dve.wait_ge(dve_step, k + 2)
                    nc.vector.tensor_tensor(mean_msg[:, j % 2, 0:n, :], acc[:, :, 0:L],
                                            spread(inv_deg[:, 1, 0:n], 2, L),
                                            ALU.mult).then_inc(dve_step, 1)
                    dve.wait_ge(dve_step, k + 3)
                    dve.wait_ge(rows_done, d * NG + (NG + j - 1))
                    nc.vector.tensor_tensor(update[:, j % 2, 0:n, :], mean_msg[:, j % 2, 0:n, :],
                                            root_sum[:, c:c + n, :], ALU.add).then_inc(update_done, 1)
                    dve.wait_ge(update_done, d * NG + (j + 1))
                    dve.sem_inc(dve_step, 1)
                nc.vector.memset(agg[:, :], 0.0)

            with dve.Fori(0, DEPTH) as d:
                root_sums(d)
                with dve.If(is_wide > 0):
                    with dve.Fori(0, ITERS) as it:
                        passes = pass_values(dve, d, it)
                        gathered = dve.snap((d * ITERS + it) * (16 * TPS) + 16 * TPS)
                        for u in range(UNROLL):
                            messages(u, passes, gathered)
                            add_wide(d, it, u)
                            split_step(u, passes)
                with dve.Else():
                    with dve.Fori(0, ITERS) as it:
                        passes = pass_values(dve, d, it)
                        gathered = dve.snap((d * ITERS + it) * (16 * TPS) + 16 * TPS)
                        _, bases = nc.values_load_multi_w_load_instructions(
                            base_sb[0:1, bass.ds(it * UNROLL, UNROLL)], engines=[mybir.EngineType.DVE],
                            min_val=0, max_val=NODES - WIN,
                            skip_runtime_bounds_check_because="window starts are node numbers")
                        for u in range(UNROLL):
                            if u % HALF == 0:
                                onehots(it, u // HALF, passes)
                            messages(u, passes, gathered)
                            if u:
                                add_window(u - 1, bases[u - 1], passes)
                            split_step(u, passes)
                        add_window(UNROLL - 1, bases[UNROLL - 1], passes)
                depth_end(d)

            dve.wait_ge(rows_done, (DEPTH + 1) * NG)
            dve.wait_ge(x_loaded, 16)
            steps[0] = n_setup + 4 * NG * DEPTH
            link(nc.vector.tensor_tensor(x_in[:, :, :], rows[:, :, :], x_in[:, :, :], ALU.add))
            link(nc.vector.tensor_reduce(stat[:, 0, :], x_in[:, :, :], AX.X, ALU.add))
            link(nc.vector.tensor_scalar(stat[:, 0, :], stat[:, 0, :], 1.0 / L, None, ALU.mult))
            link(nc.vector.tensor_tensor(x_in[:, :, :], x_in[:, :, :],
                                         spread(stat[:, 0, :], 2, L), ALU.subtract))
            link(nc.vector.tensor_tensor(squares[:, :, :], x_in[:, :, :], x_in[:, :, :], ALU.mult))
            nc.vector.tensor_reduce(stat[:, 1, :], squares[:, :, :], AX.X, ALU.add).then_inc(var_done, 1)
            dve.wait_ge(std_done, 1)
            link(nc.vector.reciprocal(stat[:, 3, :], stat[:, 2, :]))
            nc.vector.tensor_tensor(x_in[:, :, :], x_in[:, :, :],
                                    spread(stat[:, 3, :], 2, L), ALU.mult).then_inc(normed, 1)

        @block.tensor
        def _(pe):
            def layer1(s, passes, attr_passes):
                if s % HALF == 0:
                    pe.wait_ge(attr_landed[s // HALF % 2], attr_passes[s // UNROLL])
                step_done(pe, h1_done, s - 1, passes)
                nc.tensor.matmul(ps_h1[:, :], w1_sb[:, :], attr[:, s // HALF % 2, s % HALF * SE:(s % HALF + 1) * SE],
                                 start=True, stop=True).then_inc(h1_raw[s % UNROLL], 1)

            def layer2(s, passes):
                step_done(pe, h1_done, s, passes)
                step_done(pe, h2_done, s - 1, passes)
                nc.tensor.matmul(ps_h2[:, :], w2_sb[:, :], h1[:, s % 2, :],
                                 start=True, stop=True).then_inc(h2_raw[s % UNROLL], 1)

            def layer3(s, h, passes):
                half_done(pe, prod_done, s - 2, h, passes)
                nc.tensor.matmul(ps_w[:, (2 * s + h) % 4, :], b3_ones[:, :],
                                 b3_parts[:, :, :].rearrange("p t n -> p (t n)"), start=True, stop=False)
                if h == 0:
                    step_done(pe, h2_done, s, passes)
                for t in range(2):
                    last = nc.tensor.matmul(ps_w[:, (2 * s + h) % 4, t * L * L:(t + 1) * L * L],
                                            h2[:, s % 2, (2 * h + t) * P:(2 * h + t + 1) * P], w3_sb[:, :],
                                            start=False, stop=(t == 1))
                last.then_inc(w_done[2 * s + h], 1)

            def scatter(s, passes):
                step_done(pe, msg_done, s, passes)
                if s % HALF == 0:
                    pe.wait_ge(onehot_done[s // HALF], passes[0])
                step_done(pe, agg_done, s - 2, passes)
                for t in range(TPS):
                    last = nc.tensor.matmul(ps_win[0:MG, s % 2, 0:WIN], mx[:, s, t, L:MX],
                                            onehot[:, s // HALF, s % HALF * TPS + t, :],
                                            start=(t == 0), stop=(t == TPS - 1))
                last.then_inc(win_done[s], 1)

            def scatter_wide(s, n, passes):
                step_done(pe, msg_done, s, passes)
                pe.sem_inc(pe_turns, 1)
                with pe.Fori(0, NWIDE) as j:
                    pe.wait_ge(wide_onehot_done[s % HALF], n * NWIDE + j + 1)
                    for t in range(TPS):
                        last = nc.tensor.matmul(ps_win[0:MG, s % 2, :], mx[:, s, t, L:MX],
                                                wide_onehot[:, t, :], start=(t == 0), stop=(t == TPS - 1))
                    last.then_inc(wide_win_done[s % HALF], 1)
                pe.wait_ge(wide_agg_done[s % HALF], n * NWIDE + NWIDE)
                pe.sem_inc(win_done[s], 1)

            for sems in (h1_raw, h1_done, h2_raw, h2_done, w_done, prod_done, msg_done, onehot_done, win_done,
                         agg_done):
                for s in sems:
                    pe.sem_inc(s, LEAD)
            pe.wait_ge(setup_dve, 1)
            nc.tensor.matmul(ps_win[0:1, 0, 0:1], any_outside[:, :], ones[:, :], start=True, stop=True).then_inc(flag_ps, 1)
            pe.wait_ge(flag_set, 1)
            is_wide = pe.value_load(flag[0:1, 0:1], min_val=0, max_val=1 << 20)
            pe.wait_ge(w1_done, 1)
            pe.wait_ge(blocks_in, 16 * CPT)
            pe.wait_ge(rows_loaded, 16)
            pe.sem_inc(rows_done, NG)
            first = {-1: LEAD, 0: LEAD + 1}
            layer1(0, first, {0: 48})
            layer1(1, first, None)
            layer2(0, first)
            with pe.Fori(0, DEPTH) as d:
                pe.wait_ge(rows_done, d * NG + NG)
                for k, (first_t, n) in enumerate(t_banks):
                    if k >= 2:
                        pe.wait_ge(rows_t_done, d * NTB + (k - 1))
                    for a in range(n):
                        at = (first_t + a) * CPT
                        last = nc.tensor.transpose(ps_win[0:CPT * L, k % 2, a * P:(a + 1) * P],
                                                   rows[:, at:at + CPT, :].rearrange("p c i -> p (c i)"), ident[:, :])
                    last.then_inc(transposed, 1)
                for k, (first_t, n) in enumerate(t_banks):
                    pe.wait_ge(rows_t_done, d * NTB + (k + 1))
                    for a in range(n):
                        last = nc.tensor.matmul(ps_w[:, k, a * CPT * L:(a + 1) * CPT * L],
                                                rows_t[:, first_t + a, :],
                                                root_blocks[:, bass.ds(d, 1), :].rearrange("p d n -> p (d n)"),
                                                start=True, stop=True)
                    last.then_inc(root_raw, 1)
                pe.wait_ge(root_done, d * NTB + NTB)
                pe.sem_inc(pe_turns, 1)
                with pe.If(is_wide > 0):
                    with pe.Fori(0, ITERS) as it:
                        passes = pass_values(pe, d, it)
                        attr_passes = {k: (d * ITERS + it) * 48 + 48 * (k + 1) for k in (0, 1)}
                        for u in range(UNROLL):
                            layer3(u, 0, passes)
                            layer2(u + 1, passes)
                            layer3(u, 1, passes)
                            layer1(u + 2, passes, attr_passes)
                            scatter_wide(u, (d * ITERS + it) * 2 + u // HALF, passes)
                with pe.Else():
                    with pe.Fori(0, ITERS) as it:
                        passes = pass_values(pe, d, it)
                        attr_passes = {k: (d * ITERS + it) * 48 + 48 * (k + 1) for k in (0, 1)}
                        for u in range(UNROLL):
                            layer3(u, 0, passes)
                            layer2(u + 1, passes)
                            if u:
                                scatter(u - 1, passes)
                            layer3(u, 1, passes)
                            layer1(u + 2, passes, attr_passes)
                        scatter(UNROLL - 1, passes)
                pe.wait_ge(agg_done[UNROLL - 1], d * ITERS + (LEAD + ITERS))
                pe.sem_inc(pe_turns, 1)
                for j, (first_c, n) in enumerate(groups):
                    if j >= 4:
                        pe.wait_ge(update_done, d * NG + (j - 3))
                        pe.sem_inc(pe_turns, 1)
                    for c in range(n):
                        last = nc.tensor.transpose(ps_w[:, j % 4, c * MG:(c + 1) * MG],
                                                   agg[:, bass.ds(first_c + c, P, step=NB)], ident[0:MG, 0:MG])
                    last.then_inc(update_raw, 1)


def kernel(x, src, dst, edge_attr_6, L0_gnn_kW1, L0_gnn_kb1, L0_gnn_kW2, L0_gnn_kb2, L0_gnn_kW3, L0_gnn_kb3,
           L0_gnn_root_W, L0_gnn_root_b):
    import numpy as np
    import concourse.bacc as bacc
    from concourse import mybir
    from concourse.bass_utils import run_bass_kernel_spmd

    x, src, dst, edge_attr = (np.asarray(a) for a in (x, src, dst, edge_attr_6))
    n, l = x.shape
    e = src.shape[0]
    nb, iters = sizes(n, e)
    slots = iters * UNROLL * SE
    extra = 2 * UNROLL * SE

    x_rows = np.zeros((P * nb, l), x.dtype)
    x_rows[:n] = x
    attr = np.zeros((slots + extra, edge_attr.shape[1]), edge_attr.dtype)
    attr[:e] = edge_attr
    attr[slots:] = attr[:extra]
    attr_in = attr.reshape(iters + 2, UNROLL * SE, -1).transpose(0, 2, 1)
    src_pad = np.zeros(slots + extra, src.dtype)
    src_pad[:e] = src
    src_pad[slots:] = src_pad[:extra]
    src_idx = src_pad.reshape(-1, HALF * TPS, P).transpose(0, 2, 1)
    dst_pad = np.full(slots, -1, dst.dtype)
    dst_pad[:e] = dst
    dst_tiles = dst_pad.reshape(-1, P).T
    base_row = np.zeros((1, slots // SE), dst.dtype)
    first = dst_pad[::SE]
    used = -(-e // SE)
    base_row[0, :used] = first[:used]
    w3 = np.asarray(L0_gnn_kW3).reshape(-1, l, l).transpose(0, 2, 1).reshape(-1, l * l)
    arrays = dict(
        x_rows=x_rows.reshape(P, nb * l), attr_in=attr_in, src_idx=src_idx, dst_tiles=dst_tiles, base_row=base_row,
        w1=L0_gnn_kW1, b1=np.asarray(L0_gnn_kb1).reshape(-1, 1), w2=L0_gnn_kW2,
        b2=np.asarray(L0_gnn_kb2).reshape(-1, 1), w3=w3, b3=np.asarray(L0_gnn_kb3).reshape(l, l).T.reshape(1, l * l),
        root_w=L0_gnn_root_W, root_b=L0_gnn_root_b)
    arrays = {k: np.ascontiguousarray(v) for k, v in arrays.items()}

    nc = bacc.Bacc("TRN2", target_bir_lowering=False, num_devices=1)
    ins = {k: nc.dram_tensor(k, v.shape, mybir.dt.from_np(v.dtype), kind="ExternalInput").ap()
           for k, v in arrays.items()}
    out = nc.dram_tensor("out", (P, nb * l), mybir.dt.float32, kind="ExternalOutput").ap()
    gnn_resnorm_kernel(nc, **ins, out=out, n_edges=e)
    r = run_bass_kernel_spmd(nc, [arrays], core_ids=[0])
    return r.results[0]["out"].reshape(P * nb, l)[:n]
```
